# Optimizing a Trainium2 kernel written in Bass

```python
import numpy as np
import jax
import jax.numpy as jnp

def _softmax(x, axis=-1):
    return jax.nn.softmax(x, axis=axis)

def _gelu(x):
    return jax.nn.gelu(x, approximate=True)

def _silu(x):
    return jax.nn.silu(x)

def _sigmoid(x):
    return jax.nn.sigmoid(x)

def _layernorm(x, axis=-1, eps=1e-05):
    m = jnp.mean(x, axis=axis, keepdims=True)
    v = jnp.var(x, axis=axis, keepdims=True)
    return (x - m) / jnp.sqrt(v + eps)

def _scatter_add(tgt, idx, src, axis=0):
    return tgt.at[idx].add(src)

def _segment_sum(src, seg, n):
    return jax.ops.segment_sum(src, seg, n)
kernel_name = 'mk_adaln_ffn_d1_seqx_r2_ff45a4'

def setup_inputs(seed: int=0):
    np.random.seed(seed)
    _w = jnp.asarray

    def _rec_inputs():
        import jax
        import jax.numpy as jnp
        _rk = jax.random.key(seed)
        x = -0.000125 + 0.9999 * jax.random.normal(jax.random.fold_in(_rk, 1), (32, 128, 2048), jnp.float32)
        _lenS = 128 - jax.random.randint(jax.random.fold_in(_rk, 7), (32,), 0, max(1, 128 // 4) + 1, jnp.int32)
        _lenS2 = 128 - jax.random.randint(jax.random.fold_in(_rk, 8), (32,), 0, max(1, 128 // 4) + 1, jnp.int32)
        cond_128 = 0.0061147 + 1.02565 * jax.random.normal(jax.random.fold_in(_rk, 11), (32, 128), jnp.float32)
        fside_S_0 = -0.022604 + 0.987366 * jax.random.normal(jax.random.fold_in(_rk, 12), (128,), jnp.float32)
        return (x, cond_128, fside_S_0)
    x, cond_128, fside_S_0 = _rec_inputs()

    def _L0_cond_setup():
        import jax, jax.numpy as jnp
        import numpy as np
        from jax import lax
        N, C_IN, L = (32, 128, 2048)
        C_OUT, K, GROUPS = (128, 9, 4)
        C_DIM, PAD, STRIDE = (128, 4, 1)
        key = jax.random.key(seed)
        k1, k2, k3, k4, k5 = jax.random.split(key, 5)
        x = jax.random.normal(k1, (N, C_IN, L), dtype=jnp.float32)
        c = jax.random.normal(k2, (N, C_DIM), dtype=jnp.float32)
        weight = jax.random.normal(k3, (C_OUT, C_IN // GROUPS, K), dtype=jnp.float32)
        c_weight = jax.random.normal(k4, (C_OUT, C_DIM), dtype=jnp.float32)
        bias = jax.random.normal(k5, (C_OUT,), dtype=jnp.float32)
        return {'x': x, 'c': c, 'weight': weight, 'c_weight': c_weight, 'bias': bias}
    _L0_cond_all = _L0_cond_setup()
    _L0_cond_in = {k: v for k, v in _L0_cond_all.items() if k in ('weight', 'c_weight')}
    del _L0_cond_all

    def _L0_ffn_setup():
        import jax, jax.numpy as jnp
        import numpy as np
        B, T, D_IN, D_OUT = (8, 1024, 2048, 2048)
        N_LORAS, RANK = (16, 32)
        SCALING = 1.0
        key = jax.random.key(seed)
        ks = jax.random.split(key, 8)
        std = 1.0 / D_IN ** 0.5
        x = jax.random.normal(ks[0], (B, T, D_IN), dtype=jnp.float32)
        idx = jax.random.randint(ks[1], (B,), 0, N_LORAS)
        gate = jax.nn.one_hot(idx, N_LORAS, dtype=jnp.float32)
        kernel = jax.random.normal(ks[2], (D_IN, D_OUT), dtype=jnp.float32) * std
        bias = jnp.zeros((D_OUT,), dtype=jnp.float32)
        lora_A = jax.random.normal(ks[3], (N_LORAS, RANK, D_IN), dtype=jnp.float32) * std
        lora_B = jax.random.normal(ks[4], (N_LORAS, D_OUT, RANK), dtype=jnp.float32) * 0.01
        lora_A_shared = jax.random.normal(ks[5], (RANK, D_IN), dtype=jnp.float32) * std
        lora_B_shared = jax.random.normal(ks[6], (D_OUT, RANK), dtype=jnp.float32) * 0.01
        return {'x': x, 'gate': gate, 'kernel': kernel, 'bias': bias, 'lora_A': lora_A, 'lora_B': lora_B, 'lora_A_shared': lora_A_shared, 'lora_B_shared': lora_B_shared}
    _L0_ffn_all = _L0_ffn_setup()
    _L0_ffn_in = {k: v for k, v in _L0_ffn_all.items() if k in ('gate', 'kernel', 'bias', 'lora_A', 'lora_B', 'lora_A_shared', 'lora_B_shared')}
    del _L0_ffn_all
    return {'x': x, 'cond_128': cond_128, 'fside_S_0': fside_S_0, 'L0_cond_weight': _L0_cond_in['weight'], 'L0_cond_c_weight': _L0_cond_in['c_weight'], 'L0_ffn_gate': _L0_ffn_in['gate'], 'L0_ffn_kernel': _L0_ffn_in['kernel'], 'L0_ffn_bias': _L0_ffn_in['bias'], 'L0_ffn_lora_A': _L0_ffn_in['lora_A'], 'L0_ffn_lora_B': _L0_ffn_in['lora_B'], 'L0_ffn_lora_A_shared': _L0_ffn_in['lora_A_shared'], 'L0_ffn_lora_B_shared': _L0_ffn_in['lora_B_shared']}

def reference(x, cond_128, fside_S_0, L0_cond_weight, L0_cond_c_weight, L0_ffn_gate, L0_ffn_kernel, L0_ffn_bias, L0_ffn_lora_A, L0_ffn_lora_B, L0_ffn_lora_A_shared, L0_ffn_lora_B_shared):
    import jax
    import jax.numpy as jnp

    def _L0_cond_ref(x, c, weight, c_weight, bias):
        import jax, jax.numpy as jnp
        import numpy as np
        from jax import lax
        N, C_IN, L = (32, 128, 2048)
        C_OUT, K, GROUPS = (128, 9, 4)
        C_DIM, PAD, STRIDE = (128, 4, 1)
        out = lax.conv_general_dilated(x, weight, window_strides=(STRIDE,), padding=[(PAD, PAD)], dimension_numbers=('NCH', 'OIH', 'NCH'), feature_group_count=GROUPS)
        ctx = jnp.einsum('nd,od->no', c, c_weight)
        out = out + ctx[:, :, None] + bias[None, :, None]
        return out

    def _L0_ffn_ref(x, gate, kernel, bias, lora_A, lora_B, lora_A_shared, lora_B_shared):
        import jax, jax.numpy as jnp
        import numpy as np
        B, T, D_IN, D_OUT = (8, 1024, 2048, 2048)
        N_LORAS, RANK = (16, 32)
        SCALING = 1.0
        base_out = jnp.matmul(x, kernel) + bias
        b = gate.shape[0]
        x_flat = x.reshape(b, -1, x.shape[-1])
        A_eff = jnp.einsum('bn,nri->bri', gate, lora_A)
        B_eff = jnp.einsum('bn,nor->bor', gate, lora_B)
        Ax = jnp.einsum('bri,bti->btr', A_eff, x_flat)
        delta_flat = jnp.einsum('bor,btr->bto', B_eff, Ax)
        Ax_s = jnp.einsum('ri,bti->btr', lora_A_shared, x_flat)
        delta_flat = delta_flat + jnp.einsum('or,btr->bto', lora_B_shared, Ax_s)
        delta = delta_flat.reshape(x.shape[:-1] + (kernel.shape[-1],))
        return base_out + (SCALING * delta).astype(base_out.dtype)
    x = x + _L0_ffn_ref(_L0_cond_ref(x, cond_128, L0_cond_weight, L0_cond_c_weight, fside_S_0), L0_ffn_gate, L0_ffn_kernel, L0_ffn_bias, L0_ffn_lora_A, L0_ffn_lora_B, L0_ffn_lora_A_shared, L0_ffn_lora_B_shared)
    return x

_drawn_inputs = setup_inputs


def setup_inputs(seed=0):
    import zlib

    import numpy as np

    out = dict(_drawn_inputs(seed))
    spreads = {'L0_ffn_bias': (0.0, 0.8)}
    factors = {}
    for name, (base, spread) in spreads.items():
        noise = np.random.default_rng([zlib.crc32(name.encode()), seed]).standard_normal(out[name].shape)
        drawn = base * np.exp(spread * noise) if base else spread * noise
        out[name] = jnp.asarray(drawn.astype(out[name].dtype))
    for name, factor in factors.items():
        out[name] = (out[name] * factor).astype(out[name].dtype)
    return out
```

```python
from contextlib import ExitStack

import concourse.bass as bass
from concourse import mybir

F32 = mybir.dt.float32
F32R = mybir.dt.float32r
ALU = mybir.AluOpType
AX_X = mybir.AxisListType.X

P = 128
NS, CH, L = 32, 128, 2048
GR, TAPS, PAD = 4, 9, 4
GC = CH // GR
S4 = 4
HALF = L // 2
NQ = HALF // S4
QC = NQ // P
NCH = HALF // P
XW = HALF + PAD
XQ = NQ + 2
MB = L // 512
NB, RANK, NL = 8, 32, 16
SPB = NS // NB
R2 = 2 * RANK
CREDIT = 1


def build(nc, x, cond, conv_bias, conv_w, c_weight, gate, W, ffn_bias, lora_A, lora_B, lora_As, lora_Bs, out):
    mixed_A = nc.dram_tensor("mixed_A", (2, P, NCH, NB * RANK), F32, kind="Internal").ap()
    shared_A = nc.dram_tensor("shared_A", (P, 2 * NCH, RANK), F32, kind="Internal").ap()
    mixed_B = nc.dram_tensor("mixed_B", (NB * RANK, L), F32, kind="Internal").ap()
    shared_B = nc.dram_tensor("shared_B", (RANK, L), F32, kind="Internal").ap()
    partial_ax = nc.dram_tensor("partial_ax", (NS, R2, P), F32, kind="Internal").ap()

    with ExitStack() as ctx:
        def sb(name, shape, dt=F32):
            return ctx.enter_context(nc.sbuf_tensor(name, shape, dt))

        def sem(name):
            return ctx.enter_context(nc.semaphore(name))

        w_hi = sb("w_hi", [P, NCH, L], F32R)
        w_lo = sb("w_lo", [P, NCH, L], F32R)
        y_t = sb("y_t", [P, NCH, 2, P], F32R)
        stage = sb("stage", [P, 2, L])
        x_raw = sb("x_raw", [P, 4, XW])
        cv_xq = sb("cv_xq", [P, GR * NQ + GR * XQ])
        x_hi = sb("x_hi", [P, GR, XQ], F32R)
        x_lo = sb("x_lo", [P, GR, XQ], F32R)
        cw_hi = sb("cw_hi", [P, 3, GR, P], F32R)
        cw_lo = sb("cw_lo", [P, 3, GR, P], F32R)
        b_mat = sb("b_mat", [P, L])
        w_raw = sb("w_raw", [P, L])
        a_raw = sb("a_raw", [P, NCH, R2])
        a_parts = sb("a_parts", [P, NCH, 2 * R2], F32R)
        ident = sb("ident", [P, P])
        ax_tmp = sb("ax_tmp", [R2, 2 * P])
        ax = sb("ax", [P, P])
        ax_prev = sb("ax_prev", [R2, P])
        ctx_bias = sb("ctx_bias", [P, NS, GR])
        bias_col = sb("bias_col", [P, GR])
        gate_sb = sb("gate_sb", [NB, NL])
        rep = sb("rep", [P, RANK])
        gate_col = sb("gate_col", [P, NL // 4 * NB])
        acc = ctx.enter_context(nc.psum_tensor("acc", [P, MB, 512], F32))
        cps = ctx.enter_context(nc.psum_tensor("cps", [P, 4, 512], F32))

        conv_out = cv_xq[:, 0:GR * NQ].rearrange("p (g q) -> p g q", g=GR)
        x_quads = cv_xq[:, GR * NQ:].rearrange("p (g q) -> p g q", g=GR)
        w_stage = [w_raw, b_mat]
        x_flat = x_raw[:].rearrange("p s w -> p (s w)")
        y_f32 = y_t[:].bitcast(F32)
        y_hi_out = y_t[:, :, 0, :].rearrange("p k (g o) -> p g k o", g=GR)
        y_lo_out = y_t[:, :, 1, :].rearrange("p k (g o) -> p g k o", g=GR)
        y_hi_in = y_f32[:, :, 0, :].rearrange("p k (g o) -> p g k o", g=GR)
        conv_ps = cps[:, 0:2, :].rearrange("p a (g q) -> p (a g) q", q=NQ)
        turn_ps = cps[:, 2:4, :].rearrange("p a (g k) -> p (a g) k", k=NQ)
        turned = turn_ps.rearrange("p g (k o) -> p g k o", o=GC)
        ax_ps = cps[:, 2, 0:2 * P]
        W_v = W.rearrange("(h c q s) m -> h c s q m", h=2, c=QC, s=S4)

        wpad = cv_xq[:, 0:15 * GC].rearrange("p (k i) -> p k i", i=GC)
        cwT4 = cv_xq[:, 480:992]
        condT = cv_xq[:, 992:1024]
        bt = cv_xq[:, 0:1024]
        a_stage = cv_xq[:, 0:1024]
        G = cv_xq[:, 1024:2048]
        wraw = b_mat[:, 0:GC * TAPS].rearrange("p (i k) -> p k i", k=TAPS)
        cw_raw = b_mat[:, 288:416]
        cond_raw = b_mat[0:NS, 416:544]
        gate_exp = a_raw[0:NB].rearrange("p a b -> p (a b)")
        b_stage = a_raw[:].rearrange("p a b -> p (a b)")
        loraA_buf = [stage[:, 0, :], stage[:, 1, :], x_flat[:, 0:2048], x_flat[:, 2048:4096]]
        loraB_buf = [loraA_buf[1], loraA_buf[2], loraA_buf[3], loraA_buf[0]]
        As_raw = stage[0:RANK, 0, :]
        Bs_raw = stage[:, 1, 0:512]
        Bs_out = stage[:, 1, 512:1024]
        as_stage = cv_xq[:, 0:512]

        small_in = sem("small_in")
        la_raw_in = [sem(f"la_raw_in{i}") for i in range(4)]
        lb_raw_in = [sem(f"lb_raw_in{i}") for i in range(4)]
        as_raw_in = sem("as_raw_in")
        bs_raw_in = sem("bs_raw_in")
        id_ready = sem("id_ready")
        wpad_zero = sem("wpad_zero")
        wpad_ready = sem("wpad_ready")
        gexp_ready = sem("gexp_ready")
        rep_ready = sem("rep_ready")
        cwt_done = sem("cwt_done")
        ctxt_done = sem("ctxt_done")
        ctxt_ready = sem("ctxt_ready")
        gcol_done = sem("gcol_done")
        gcol_ready = sem("gcol_ready")
        ctx_done = sem("ctx_done")
        ctx_ready = sem("ctx_ready")
        g_ready = sem("g_ready")
        cw_hi_ready = sem("cw_hi_ready")
        cw_lo_ready = sem("cw_lo_ready")
        amix_done = sem("amix_done")
        amix_copied = sem("amix_copied")
        amix_out = sem("amix_out")
        as_done = sem("as_done")
        as_copied = sem("as_copied")
        as_out = sem("as_out")
        bt_done = sem("bt_done")
        bt_ready = sem("bt_ready")
        bmix_done = sem("bmix_done")
        bmix_copied = sem("bmix_copied")
        bmix_out = sem("bmix_out")
        bs_done = sem("bs_done")
        bs_copied = sem("bs_copied")
        bs_out = sem("bs_out")
        edge_zero = sem("edge_zero")
        w_in = [sem("w_in0"), sem("w_in1")]
        w_hi_ready = sem("w_hi_ready")
        w_lo_ready = sem("w_lo_ready")
        w_chunk_used = sem("w_chunk_used")
        x_in = [sem(f"x_in{i}") for i in range(4)]
        xq_act = sem("xq_act")
        xq_dve = sem("xq_dve")
        x_hi_ready = sem("x_hi_ready")
        x_lo_ready = sem("x_lo_ready")
        conv_done = sem("conv_done")
        conv_copied = sem("conv_copied")
        turn_done = sem("turn_done")
        y_hi_ready = sem("y_hi_ready")
        y_lo_ready = sem("y_lo_ready")
        a_in = sem("a_in")
        as_in = sem("as_in")
        a_hi_ready = sem("a_hi_ready")
        a_lo_ready = sem("a_lo_ready")
        ax_done = sem("ax_done")
        ax_upper = sem("ax_upper")
        ax_sum = sem("ax_sum")
        ax_ready = sem("ax_ready")
        ax_stored = sem("ax_stored")
        axp_in = sem("axp_in")
        bs_in = sem("bs_in")
        b_in = sem("b_in")
        ffn_done = sem("ffn_done")
        out_dve = sem("out_dve")
        out_act = sem("out_act")
        stored = [sem("stored0"), sem("stored1")]
        part_in = [sem("part_in0"), sem("part_in1")]
        pre_added = sem("pre_added")

        def credit(eng, *sems_and_steps):
            for s, n in sems_and_steps:
                eng.sem_inc(s, n)

        def phases(eng, step):
            for ph in range(2):
                with eng.Fori(0, NB - 1) as i:
                    for j in range(SPB):
                        step(i, ph, j)
                for j in range(SPB):
                    step(NB - 1, ph, j)

        def load_x(eng, n, ph, slot):
            src = x[n][:, 0:XW] if ph == 0 else x[n][:, L - XW:L]
            eng.dma_start(x_raw[:, slot, :], src).then_inc(x_in[slot], 16)

        block = ctx.enter_context(nc.Block())

        @block.sync
        def _(sp):
            credit(sp, (stored[0], 16), (stored[1], 16), (ax_stored, 16))
            sp.dma_start(b_mat[:, 0:GC * TAPS], conv_w.rearrange("o i k -> o (i k)")).then_inc(small_in, 16)
            sp.dma_start(cw_raw, c_weight).then_inc(small_in, 16)
            sp.dma_start(cond_raw, cond).then_inc(small_in, 16)
            sp.dma_start(gate_sb[:], gate).then_inc(small_in, 16)
            with nc.allow_non_contiguous_dma(reason="128 bias values, one per partition"):
                for s in range(S4):
                    sp.dma_start(bias_col[s * GC:(s + 1) * GC, :],
                                 conv_bias.rearrange("(g o) -> o g", g=GR)).then_inc(small_in, 16)
            for k in range(4):
                sp.dma_start(loraA_buf[k], lora_A[4 * k:4 * k + 4].rearrange("n r l -> (n r) l")).then_inc(la_raw_in[k], 16)
            for k in range(4):
                sp.wait_ge(amix_copied, k + 1)
                sp.dma_start(mixed_A[k // 2, :, 4 * (k % 2):4 * (k % 2) + 4, :],
                             a_stage.rearrange("p (k n) -> p k n", k=4)).then_inc(amix_out, 16)
                if k == 3:
                    sp.dma_start(As_raw, lora_As).then_inc(as_raw_in, 16)

            def load_lora_B(k):
                for m in range(4):
                    sp.dma_start(loraB_buf[k][:, 512 * m:512 * m + 512].rearrange("p (n r) -> p n r", r=RANK),
                                 lora_B[:, (4 * k + m) * P:(4 * k + m + 1) * P, :].rearrange("n p r -> p n r")
                                 ).then_inc(lb_raw_in[k], 16)

            for k in range(3):
                load_lora_B(k)
            sp.wait_ge(as_done, 1)
            load_lora_B(3)
            sp.wait_ge(as_copied, 1)
            sp.dma_start(shared_A, as_stage.rearrange("p (k r) -> p k r", r=RANK)).then_inc(as_out, 16)
            for k in range(8):
                sp.wait_ge(bmix_copied, k + 1)
                sp.dma_start(mixed_B.rearrange("(t p) m -> p t m", p=P)[:, :, 256 * k:256 * k + 256],
                             b_stage.rearrange("p (t m) -> p t m", t=2)).then_inc(bmix_out, 16)
                if k == 1:
                    sp.dma_start(Bs_raw.rearrange("p (k r) -> p k r", r=RANK),
                                 lora_Bs.rearrange("(k p) r -> p k r", p=P)).then_inc(bs_raw_in, 16)
                if k == 3:
                    load_x(sp, 0, 0, 0)
                if k == 5:
                    load_x(sp, 1, 0, 1)
                    load_x(sp, 2, 0, 2)
            sp.wait_ge(bs_copied, 1)
            for k in range(4):
                sp.dma_start(shared_B.rearrange("r (j k m) -> k r j m", k=4, m=P)[k],
                             Bs_out[k * RANK:(k + 1) * RANK].rearrange("r (j m) -> r j m", m=P)).then_inc(bs_out, 16)
            sp.wait_ge(amix_out, 64)
            sp.wait_ge(as_out, 16)
            sp.wait_ge(bmix_out, 128)
            sp.dma_start(a_raw[:, :, RANK:R2], shared_A[:, 0:NCH, :]).then_inc(as_in, 16)
            sp.dma_start(a_raw[:, :, 0:RANK], mixed_A[0, :, :, 0:RANK]).then_inc(a_in, 16)

            def step(i, ph, j):
                t = 32 * ph + 4 * i + j
                n = 4 * i + j
                last = type(i) is int
                if ph == 1 and not (last and j == 3):
                    sp.wait_ge(stored[(j + 1) % 2], 16 * (CREDIT + 16 * ph + 2 * i + (j + 1) // 2))
                sp.wait_ge(out_dve, CREDIT + t)
                if not (last and j >= 1):
                    load_x(sp, n + 3, ph, (j + 3) % 4)
                elif ph == 0:
                    load_x(sp, j - 1, 1, (j + 3) % 4)
                if ph == 0:
                    sp.wait_ge(ax_ready, CREDIT + t + 1)
                    sp.dma_start(partial_ax[n], ax[0:R2, :]).then_inc(ax_stored, 16)
                elif not (last and j == 3):
                    sp.wait_ge(ax_ready, CREDIT + t + 1)
                    sp.dma_start(ax_prev[:], partial_ax[n + 1]).then_inc(axp_in, 16)
                    sp.dma_start(stage[:, (j + 1) % 2, :], out[n + 1]).then_inc(part_in[(j + 1) % 2], 16)
                if ph == 1 and j == 0:
                    sp.dma_start(b_mat[0:RANK, :], mixed_B.rearrange("(b r) m -> b r m", r=RANK)[i]).then_inc(b_in, 16)
                if j == 0 and not (last and ph == 1):
                    sp.wait_ge(a_lo_ready, 8 * ph + i + 1)
                    if last:
                        sp.dma_start(a_raw[:, :, RANK:R2], shared_A[:, NCH:2 * NCH, :]).then_inc(as_in, 16)
                        sp.dma_start(a_raw[:, :, 0:RANK], mixed_A[1, :, :, 0:RANK]).then_inc(a_in, 16)
                    else:
                        sp.dma_start(a_raw[:, :, 0:RANK],
                                     mixed_A[ph].rearrange("p k (b r) -> b p k r", r=RANK)[i + 1]).then_inc(a_in, 16)
                sp.wait_ge(out_dve, CREDIT + t + 1)
                if ph == 0:
                    sp.wait_ge(out_act, CREDIT + t + 1)
                sp.dma_start(out[n], stage[:, j % 2, :]).then_inc(stored[j % 2], 16)
                if ph == 0 and last and j == 3:
                    sp.wait_ge(stored[0], 16 * (CREDIT + 16))
                    sp.dma_start(stage[:, 0, :], out[0]).then_inc(part_in[0], 16)
                    sp.wait_ge(ax_stored, 16 * (CREDIT + NS))
                    sp.dma_start(ax_prev[:], partial_ax[0]).then_inc(axp_in, 16)
                    sp.wait_ge(w_lo_ready, 2 * NCH)
                    sp.wait_ge(bs_out, 64)
                    sp.dma_start(b_mat[RANK:R2, :], shared_B).then_inc(bs_in, 16)
                    sp.dma_start(b_mat[R2:R2 + 1, :], ffn_bias.rearrange("(a m) -> a m", a=1)).then_inc(bs_in, 16)

            phases(sp, step)
            sp.wait_ge(stored[0], 16 * (CREDIT + NS))
            sp.wait_ge(stored[1], 16 * (CREDIT + NS))

        @block.gpsimd
        def _(pool):
            nc.gpsimd.memset(ident[:], 0.0).then_inc(id_ready, 1)
            pool.wait_ge(id_ready, 1)
            nc.gpsimd.affine_select(out=ident[:], in_=ident[:], compare_op=ALU.not_equal, fill=1.0, base=0,
                                    pattern=[[-1, P]], channel_multiplier=1).then_inc(id_ready, 1)
            pool.wait_ge(id_ready, 2)
            nc.gpsimd.memset(ax[R2:R2 + 1, :], 1.0).then_inc(id_ready, 1)
            pool.wait_ge(id_ready, 3)

            def step(i, ph, j):
                t = 4 * i + j
                pool.wait_ge(x_in[j], 16 * (8 + i + 1))
                pool.wait_ge(part_in[j % 2], 16 * (2 * i + j // 2 + 1))
                nc.gpsimd.tensor_tensor(stage[:, j % 2, HALF:L], stage[:, j % 2, HALF:L],
                                        x_raw[:, j, PAD:XW], ALU.add).then_inc(pre_added, 1)

            with pool.Fori(0, NB) as i:
                for j in range(SPB):
                    step(i, 1, j)

        @block.scalar
        def _(act):
            credit(act, (out_act, 1))

            def load_w(k):
                if k >= 2:
                    act.wait_ge(w_lo_ready, k - 1)
                act.dma_start(w_stage[k % 2][:], W_v[k // NCH, k % NCH // S4, k % S4]).then_inc(w_in[k % 2], 16)

            def split_w(k):
                act.wait_ge(w_in[k % 2], 16 * (k // 2 + 1))
                if k == 2 * NCH - 1:
                    act.wait_ge(ffn_done, NS)
                elif k >= NCH:
                    act.wait_ge(w_chunk_used, k % NCH + 1)
                nc.scalar.copy(w_hi[:, k % NCH, :], w_stage[k % 2][:]).then_inc(w_hi_ready, 1)

            def x_rearrange(slot, in_value, t_plus_1, ph, first=False):
                act.wait_ge(x_in[slot], in_value)
                if not first:
                    act.wait_ge(x_lo_ready, t_plus_1 - 1)
                else:
                    act.wait_ge(edge_zero, 1)
                for g in range(2):
                    for r in range(S4):
                        ins = nc.scalar.copy(x_quads[r * GC:(r + 1) * GC, g, 1 - ph:1 - ph + NQ + 1],
                                             x_raw[g * GC:(g + 1) * GC, slot, r:XW:S4])
                ins.then_inc(xq_act, 1)

            def x_split(t_plus_1, first=False):
                act.wait_ge(xq_act, t_plus_1)
                act.wait_ge(xq_dve, t_plus_1)
                if not first:
                    act.wait_ge(conv_done, t_plus_1 - 1)
                nc.scalar.copy(x_hi[:], x_quads).then_inc(x_hi_ready, 1)

            def y_split(t_plus_1):
                act.wait_ge(turn_done, t_plus_1)
                nc.scalar.copy(y_hi_out, turned).then_inc(y_hi_ready, 1)

            def a_split(k_plus_1, as_value):
                act.wait_ge(a_in, 16 * k_plus_1)
                act.wait_ge(as_in, as_value)
                nc.scalar.copy(a_parts[:, :, 0:R2], a_raw[:]).then_inc(a_hi_ready, 1)

            load_w(0)
            act.wait_ge(cwt_done, 1)
            for d in range(3):
                ins = nc.scalar.copy(cw_hi[:, d].rearrange("p g (s o) -> p s g o", s=S4),
                                     cps[:, d, :].rearrange("p (s g o) -> p s g o", s=S4, g=GR))
            ins.then_inc(cw_hi_ready, 1)
            act.wait_ge(ctxt_done, 1)
            load_w(1)
            for k in range(NCH):
                split_w(k)
                if k + 2 < NCH:
                    load_w(k + 2)
            for k in range(8):
                act.wait_ge(bt_done, k + 1)
                if k == 0:
                    act.wait_ge(amix_out, 64)
                    act.wait_ge(as_out, 16)
                else:
                    act.wait_ge(bmix_done, k)
                nc.scalar.copy(bt, acc[:, 0:2, :].rearrange("p a n -> p (a n)")).then_inc(bt_ready, 1)
            x_rearrange(0, 16, 1, 0, first=True)
            x_split(1, first=True)
            x_rearrange(1, 16, 2, 0)
            x_split(2)
            y_split(1)
            a_split(1, 16)

            def step(i, ph, j):
                t = 32 * ph + 4 * i + j
                last = type(i) is int
                act.wait_ge(ax_done, t + 1)
                act.wait_ge(ax_ready, CREDIT + t)
                nc.scalar.copy(ax_tmp[:], ax_ps[R2:P, :]).then_inc(ax_upper, 1)
                if ph == 0 and last and j == 2:
                    load_w(NCH)
                    load_w(NCH + 1)
                more = not (ph == 1 and last)
                if more or j < 2:
                    nph = 1 if last and j >= 2 else ph
                    x_rearrange((j + 2) % 4, 16 * (8 * ph + i + (j + 2) // 4 + 1), t + 3, nph)
                    x_split(t + 3)
                if j == 3 and more:
                    a_split(8 * ph + i + 2, 32 if last or ph == 1 else 16)
                if ph == 0 and last and j == 3:
                    for k in range(NCH, 2 * NCH):
                        split_w(k)
                        if k + 2 < 2 * NCH:
                            load_w(k + 2)
                if ph == 0:
                    act.wait_ge(ffn_done, t + 1)
                    act.wait_ge(stored[j % 2], 16 * (CREDIT + 2 * i + j // 2))
                    nc.scalar.copy(stage[:, j % 2, HALF:L], acc[:, 2:4, :].rearrange("p a n -> p (a n)")
                                   ).then_inc(out_act, 1)
                if more or j < 3:
                    y_split(t + 2)

            phases(act, step)

        @block.vector
        def _(dve):
            credit(dve, (out_dve, 1), (ax_ready, 1))
            V = nc.vector

            def split_w(k):
                dve.wait_ge(w_hi_ready, k + 1)
                V.tensor_tensor(w_lo[:, k % NCH, :], w_stage[k % 2][:], w_hi[:, k % NCH, :].bitcast(F32),
                                ALU.subtract).then_inc(w_lo_ready, 1)

            def x_rearrange(slot, in_value, t_plus_1, ph, first=False):
                dve.wait_ge(x_in[slot], in_value)
                if not first:
                    dve.wait_ge(x_hi_ready, t_plus_1 - 1)
                    dve.wait_ge(x_lo_ready, t_plus_1 - 1)
                for g in range(2, GR):
                    for r in range(S4):
                        ins = V.tensor_copy(x_quads[r * GC:(r + 1) * GC, g, 1 - ph:1 - ph + NQ + 1],
                                            x_raw[g * GC:(g + 1) * GC, slot, r:XW:S4])
                ins.then_inc(xq_dve, 1)

            def x_split(t_plus_1):
                dve.wait_ge(xq_dve, t_plus_1)
                dve.wait_ge(x_hi_ready, t_plus_1)
                V.tensor_tensor(x_lo[:], x_quads, x_hi[:].bitcast(F32), ALU.subtract).then_inc(x_lo_ready, 1)

            def conv_copy(n, t_plus_1):
                dve.wait_ge(conv_done, t_plus_1)
                bias = ctx_bias[:, n, :].unsqueeze(2).to_broadcast([P, GR, NQ])
                V.tensor_tensor(conv_out, conv_ps, bias, ALU.add).then_inc(conv_copied, 1)

            def y_split(t_plus_1):
                dve.wait_ge(y_hi_ready, t_plus_1)
                V.tensor_tensor(y_lo_out, turned, y_hi_in, ALU.subtract).then_inc(y_lo_ready, 1)

            def a_split(k_plus_1):
                dve.wait_ge(a_hi_ready, k_plus_1)
                V.tensor_tensor(a_parts[:, :, R2:2 * R2], a_raw[:], a_parts[:, :, 0:R2].bitcast(F32),
                                ALU.subtract).then_inc(a_lo_ready, 1)

            V.memset(wpad, 0.0).then_inc(wpad_zero, 1)
            dve.wait_ge(small_in, 16 * 8)
            dve.wait_ge(wpad_zero, 1)
            V.tensor_copy(wpad[:, 3:3 + TAPS, :], wraw).then_inc(wpad_ready, 1)
            V.tensor_copy(gate_exp.rearrange("b (n r) -> b n r", r=RANK),
                          gate_sb[:].unsqueeze(2).to_broadcast([NB, NL, RANK])).then_inc(gexp_ready, 1)
            dve.wait_ge(id_ready, 2)
            V.tensor_reduce(rep[:], ident[:].rearrange("p (a r) -> p r a", r=RANK), AX_X, ALU.add).then_inc(rep_ready, 1)
            dve.wait_ge(ctxt_done, 1)
            V.tensor_copy(cwT4.rearrange("p (g s o) -> p g s o", g=GR, s=S4),
                          acc[:, 0, 0:CH].rearrange("p (g o) -> p g o", g=GR).unsqueeze(2).to_broadcast([P, GR, S4, GC])
                          ).then_inc(ctxt_ready, 1)
            V.tensor_copy(condT, acc[:, 0, CH:CH + NS]).then_inc(ctxt_ready, 1)
            dve.wait_ge(gcol_done, 1)
            V.tensor_copy(gate_col[:], acc[:, 1, 0:32]).then_inc(gcol_ready, 1)
            dve.wait_ge(gcol_ready, 1)
            dve.wait_ge(rep_ready, 1)
            V.tensor_tensor(G.rearrange("p (c r) -> p c r", r=RANK),
                            gate_col[:].unsqueeze(2).to_broadcast([P, 32, RANK]),
                            rep[:].unsqueeze(1).to_broadcast([P, 32, RANK]), ALU.mult).then_inc(g_ready, 1)
            dve.wait_ge(ctx_done, 1)
            V.tensor_tensor(ctx_bias[:].rearrange("p n g -> p g n"),
                            acc[:, 2, 0:P].rearrange("p (g n) -> p g n", g=GR),
                            bias_col[:].unsqueeze(2).to_broadcast([P, GR, NS]), ALU.add).then_inc(ctx_ready, 1)
            dve.wait_ge(cw_hi_ready, 1)
            for d in range(3):
                ins = V.tensor_tensor(cw_lo[:, d].rearrange("p g (s o) -> p s g o", s=S4),
                                      cps[:, d, :].rearrange("p (s g o) -> p s g o", s=S4, g=GR),
                                      cw_hi[:, d].bitcast(F32).rearrange("p g (s o) -> p s g o", s=S4), ALU.subtract)
            ins.then_inc(cw_lo_ready, 1)
            for k in range(4):
                split_w(k)
            for k in range(4):
                dve.wait_ge(amix_done, k + 1)
                if k:
                    dve.wait_ge(amix_out, 16 * k)
                else:
                    dve.wait_ge(ctx_done, 1)
                V.tensor_copy(a_stage, cps[:, 2 * (k % 2):2 * (k % 2) + 2, :].rearrange("p a n -> p (a n)")
                              ).then_inc(amix_copied, 1)
                split_w(4 + k)
            dve.wait_ge(as_done, 1)
            dve.wait_ge(amix_out, 64)
            V.tensor_copy(as_stage, acc[:, 3, :]).then_inc(as_copied, 1)
            for k in range(8):
                dve.wait_ge(bmix_done, k + 1)
                if k:
                    dve.wait_ge(bmix_out, 16 * k)
                V.tensor_copy(b_stage, cps[:, k % 2, :]).then_inc(bmix_copied, 1)
            dve.wait_ge(bs_done, 1)
            V.tensor_copy(Bs_out, acc[:, 2, :]).then_inc(bs_copied, 1)
            V.memset(x_quads[:, :, 0:1], 0.0).then_inc(edge_zero, 1)
            x_rearrange(0, 16, 1, 0, first=True)
            dve.wait_ge(edge_zero, 1)
            x_split(1)
            x_rearrange(1, 16, 2, 0)
            dve.wait_ge(conv_done, 1)
            x_split(2)
            conv_copy(0, 1)
            y_split(1)
            a_split(1)

            def step(i, ph, j):
                t = 32 * ph + 4 * i + j
                n = 4 * i + j
                last = type(i) is int
                more = not (ph == 1 and last)
                if more or j < 3:
                    conv_copy((n + 1) if not (last and j == 3) else 0, t + 2)
                dve.wait_ge(ax_upper, t + 1)
                V.tensor_tensor(ax_tmp[:], ax_ps[0:R2, :], ax_tmp[:], ALU.add).then_inc(ax_sum, 1)
                dve.wait_ge(ax_sum, t + 1 if ph == 0 else NS + 2 * n + 1)
                if ph == 0:
                    dve.wait_ge(ax_stored, 16 * (CREDIT + t))
                    V.tensor_tensor(ax[0:R2, :], ax_tmp[:, 0:P], ax_tmp[:, P:2 * P], ALU.add).then_inc(ax_ready, 1)
                else:
                    V.tensor_tensor(ax_tmp[:, 0:P], ax_tmp[:, 0:P], ax_tmp[:, P:2 * P], ALU.add).then_inc(ax_sum, 1)
                    dve.wait_ge(axp_in, 16 * (4 * i + j + 1))
                    dve.wait_ge(ax_stored, 16 * (CREDIT + NS))
                    dve.wait_ge(ax_sum, NS + 2 * (4 * i + j) + 2)
                    V.tensor_tensor(ax[0:R2, :], ax_tmp[:, 0:P], ax_prev[:], ALU.add).then_inc(ax_ready, 1)
                if more or j < 2:
                    nph = 1 if last and j >= 2 else ph
                    if ph == 0 and last and j == 2:
                        dve.wait_ge(x_hi_ready, t + 2)
                        dve.wait_ge(x_lo_ready, t + 2)
                        V.memset(x_quads[:, :, XQ - 1:XQ], 0.0).then_inc(edge_zero, 1)
                    x_rearrange((j + 2) % 4, 16 * (8 * ph + i + (j + 2) // 4 + 1), t + 3, nph)
                    if ph == 0 and last and j == 2:
                        dve.wait_ge(edge_zero, 2)
                    x_split(t + 3)
                if j == 3 and more:
                    a_split(8 * ph + i + 2)
                if ph == 0 and last and j == 3:
                    for k in range(NCH, 2 * NCH):
                        split_w(k)
                dve.wait_ge(ffn_done, t + 1)
                if ph == 0:
                    dve.wait_ge(stored[j % 2], 16 * (CREDIT + 2 * i + j // 2))
                    V.tensor_tensor(stage[:, j % 2, 0:HALF], acc[:, 0:2, :].rearrange("p a n -> p (a n)"),
                                    x_raw[:, j, 0:HALF], ALU.add).then_inc(out_dve, 1)
                else:
                    dve.wait_ge(pre_added, 4 * i + j + 1)
                    V.tensor_tensor(stage[:, j % 2, :], acc[:].rearrange("p a n -> p (a n)"), stage[:, j % 2, :],
                                    ALU.add).then_inc(out_dve, 1)
                if more or j < 3:
                    y_split(t + 2)

            phases(dve, step)

        @block.tensor
        def _(pe):
            T = nc.tensor

            def conv(t_plus_1):
                pe.wait_ge(x_lo_ready, t_plus_1)
                for g in range(GR):
                    n = 0
                    for d in range(3):
                        for wt, xt in ((cw_hi, x_hi), (cw_hi, x_lo), (cw_lo, x_hi)):
                            ins = T.matmul(conv_ps[:, g, :], wt[:, d, g, :], xt[:, g, d:d + NQ],
                                           start=(n == 0), stop=(n == 8))
                            n += 1
                ins.then_inc(conv_done, 1)

            def turn(t_plus_1):
                pe.wait_ge(conv_copied, t_plus_1)
                for g in range(GR):
                    for c in range(QC):
                        ins = T.transpose(turn_ps[:, g, c * P:(c + 1) * P], conv_out[:, g, c * P:(c + 1) * P],
                                          ident[:])
                ins.then_inc(turn_done, 1)

            pe.wait_ge(id_ready, 3)
            pe.wait_ge(wpad_ready, 1)
            wp = wpad.rearrange("p k i -> p (k i)")
            for d in range(3):
                for s in range(S4):
                    k0 = (4 * d + 3 - s) * GC
                    ins = T.transpose(cps[:, d, s * P:(s + 1) * P], wp[:, k0:k0 + P], ident[:])
            ins.then_inc(cwt_done, 1)
            pe.wait_ge(small_in, 16 * 8)
            T.transpose(acc[:, 0, 0:CH], cw_raw, ident[:])
            T.transpose(acc[:, 0, CH:CH + NS], cond_raw, ident[0:NS, 0:NS]).then_inc(ctxt_done, 1)
            pe.wait_ge(gexp_ready, 1)
            for k in range(4):
                ins = T.matmul(acc[:, 1, k * NB:(k + 1) * NB], gate_exp[:, k * P:(k + 1) * P], ident[0:NB, 0:NB],
                               start=True, stop=True)
            ins.then_inc(gcol_done, 1)
            pe.wait_ge(ctxt_ready, 2)
            for g in range(GR):
                ins = T.matmul(acc[:, 2, g * NS:(g + 1) * NS], cwT4[:, g * P:(g + 1) * P], condT, start=True, stop=True)
            ins.then_inc(ctx_done, 1)
            pe.wait_ge(g_ready, 1)
            pe.wait_ge(cw_lo_ready, 1)
            for k in range(4):
                pe.wait_ge(la_raw_in[k], 16)
            for k in range(4):
                if k >= 2:
                    pe.wait_ge(amix_copied, k - 1)
                for c in range(4):
                    ch = 4 * k + c
                    l0 = ch // S4 * 512 + ch % S4
                    dst = cps[:, 2 * (k % 2) + c // 2, (c % 2) * 256:(c % 2) * 256 + 256]
                    for b in range(4):
                        ins = T.matmul(dst, loraA_buf[b][:, l0:l0 + 509:S4], G[:, b * 256:(b + 1) * 256],
                                       start=(b == 0), stop=(b == 3))
                ins.then_inc(amix_done, 1)
            pe.wait_ge(as_raw_in, 16)
            for ch in range(2 * NCH):
                l0 = ch // S4 * 512 + ch % S4
                ins = T.transpose(acc[:, 3, ch * RANK:(ch + 1) * RANK], As_raw[:, l0:l0 + 509:S4], ident[0:RANK, 0:RANK])
            ins.then_inc(as_done, 1)
            pe.wait_ge(amix_copied, 4)
            for k in range(8):
                pe.wait_ge(lb_raw_in[k // 2], 64)
                if k:
                    pe.wait_ge(bt_ready, k)
                else:
                    pe.wait_ge(gcol_ready, 1)
                for b in range(4):
                    for m in range(2):
                        raw = loraB_buf[k // 2][:, (2 * (k % 2) + m) * 512 + b * P:(2 * (k % 2) + m) * 512 + (b + 1) * P]
                        col = b * 256 + m * P
                        ins = T.transpose(acc[:, col // 512, col % 512:col % 512 + P], raw, ident[:])
                ins.then_inc(bt_done, 1)
                pe.wait_ge(bt_ready, k + 1)
                if k >= 2:
                    pe.wait_ge(bmix_copied, k - 1)
                for h in range(2):
                    for b in range(4):
                        ins = T.matmul(cps[:, k % 2, h * 256:(h + 1) * 256], G[:, b * 256 + h * P:b * 256 + (h + 1) * P],
                                       bt[:, b * 256:(b + 1) * 256], start=(b == 0), stop=(b == 3))
                ins.then_inc(bmix_done, 1)
            pe.wait_ge(bs_raw_in, 16)
            for k in range(4):
                ins = T.transpose(acc[:, 2, k * P:(k + 1) * P], Bs_raw[:, k * P:(k + 1) * P], ident[:])
            ins.then_inc(bs_done, 1)
            pe.wait_ge(bmix_copied, 8)
            conv(1)
            turn(1)
            conv(2)

            def step(i, ph, j):
                t = 32 * ph + 4 * i + j
                last = type(i) is int
                more = not (ph == 1 and last)
                if j == 0:
                    pe.wait_ge(a_lo_ready, 8 * ph + i + 1)
                pe.wait_ge(y_lo_ready, t + 1)
                for ch in range(NCH):
                    ins = T.matmul(ax_ps, a_parts[:, ch, :], y_t[:, ch].rearrange("p h r -> p (h r)"),
                                   start=(ch == 0), stop=(ch == NCH - 1))
                ins.then_inc(ax_done, 1)
                pe.wait_ge(out_dve, CREDIT + t)
                if ph == 0:
                    pe.wait_ge(out_act, CREDIT + t)
                elif j == 0:
                    pe.wait_ge(out_act, CREDIT + NS)
                for ch in range(NCH):
                    if j == 0:
                        pe.wait_ge(w_lo_ready, NCH * ph + ch + 1)
                    for part, wt in ((0, w_hi), (0, w_lo), (1, w_hi)):
                        for m in range(MB):
                            ins = T.matmul(acc[:, m, :], y_t[:, ch, part, :], wt[:, ch, m * 512:(m + 1) * 512],
                                           start=(ch == 0 and part == 0 and wt is w_hi),
                                           stop=(ph == 0 and ch == NCH - 1 and part == 1))
                    if ph == 0 and last and j == 3:
                        if ch < NCH - 1:
                            ins.then_inc(w_chunk_used, 1)
                if ph == 0:
                    ins.then_inc(ffn_done, 1)
                else:
                    pe.wait_ge(ax_ready, CREDIT + t + 1)
                    if j == 0:
                        pe.wait_ge(bs_in, 32)
                        pe.wait_ge(b_in, 16 * (i + 1))
                    for m in range(MB):
                        ins = T.matmul(acc[:, m, :], ax[0:R2 + 1, :], b_mat[0:R2 + 1, m * 512:(m + 1) * 512],
                                       start=False, stop=True)
                    ins.then_inc(ffn_done, 1)
                if more or j < 3:
                    pe.wait_ge(ax_ready, CREDIT + t + 1)
                    turn(t + 2)
                if more or j < 2:
                    conv(t + 3)

            phases(pe, step)


INPUTS = ["x", "cond_128", "fside_S_0", "L0_cond_weight", "L0_cond_c_weight", "L0_ffn_gate", "L0_ffn_kernel",
          "L0_ffn_bias", "L0_ffn_lora_A", "L0_ffn_lora_B", "L0_ffn_lora_A_shared", "L0_ffn_lora_B_shared"]


def kernel(**inputs):
    import numpy as np
    import concourse.bacc as bacc
    from concourse.bass_utils import run_bass_kernel_spmd

    nc = bacc.Bacc("TRN2", target_bir_lowering=False, num_devices=1, dynamic_dma_scratch_size=1024)
    arrays, aps = {}, []
    for name in INPUTS:
        a = np.ascontiguousarray(inputs[name])
        arrays[f"in_{name}"] = a
        aps.append(nc.dram_tensor(f"in_{name}", a.shape, mybir.dt.from_np(a.dtype), kind="ExternalInput").ap())
    out = nc.dram_tensor("out", (NS, CH, L), F32, kind="ExternalOutput").ap()
    build(nc, *aps, out)
    r = run_bass_kernel_spmd(nc, [arrays], core_ids=[0])
    return r.results[0]["out"]
```

```python
from contextlib import ExitStack

import concourse.bass as bass
from concourse import mybir

F32 = mybir.dt.float32
F32R = mybir.dt.float32r
ALU = mybir.AluOpType
AX_X = mybir.AxisListType.X

P = 128
NS, CH, L = 32, 128, 2048
GR, TAPS, PAD = 4, 9, 4
GC = CH // GR
S4 = 4
HALF = L // 2
NQ = HALF // S4
QC = NQ // P
NCH = HALF // P
XW = HALF + PAD
XQ = NQ + 2
MB = L // 512
NB, RANK, NL = 8, 32, 16
SPB = NS // NB
R2 = 2 * RANK
W_EARLY = 6
R8 = P // NL
RK = RANK // R8
CREDIT = 1


def build(nc, x, cond, conv_bias, conv_w, c_weight, gate, W, ffn_bias, lora_A, lora_B, lora_As, lora_Bs, out):
    mixed_A = nc.dram_tensor("mixed_A", (2, P, NCH, NB * RANK), F32, kind="Internal").ap()
    mixed_B = nc.dram_tensor("mixed_B", (NB * R8, RK, L), F32, kind="Internal").ap()
    shared_B = nc.dram_tensor("shared_B", (RANK, L), F32, kind="Internal").ap()
    partial_ax = nc.dram_tensor("partial_ax", (NS, R2, P), F32, kind="Internal").ap()

    with ExitStack() as ctx:
        def sb(name, shape, dt=F32):
            return ctx.enter_context(nc.sbuf_tensor(name, shape, dt))

        def sem(name):
            return ctx.enter_context(nc.semaphore(name))

        w_hi = sb("w_hi", [P, NCH, L], F32R)
        w_lo = sb("w_lo", [P, NCH, L], F32R)
        y_t = sb("y_t", [P, NCH, 2, P], F32R)
        stage = sb("stage", [P, 2, L])
        x_raw = sb("x_raw", [P, 4, XW])
        cv_xq = sb("cv_xq", [P, GR * NQ + GR * XQ])
        x_hi = sb("x_hi", [P, GR, XQ], F32R)
        x_lo = sb("x_lo", [P, GR, XQ], F32R)
        cw_hi = sb("cw_hi", [P, 3, GR, P], F32R)
        cw_lo = sb("cw_lo", [P, 3, GR, P], F32R)
        b_mat = sb("b_mat", [P, L])
        w_raw = sb("w_raw", [P, L])
        a_raw = sb("a_raw", [P, NCH, R2])
        a_parts = sb("a_parts", [P, NCH, 2 * R2], F32R)
        ident = sb("ident", [P, P])
        ax_tmp = sb("ax_tmp", [R2, 2 * P])
        ax = sb("ax", [P, P])
        ax_prev = sb("ax_prev", [R2, P])
        ctx_bias = sb("ctx_bias", [P, NS, GR])
        bias_col = sb("bias_col", [P, GR])
        gate_sb = sb("gate_sb", [NB, NL])
        rep = sb("rep", [P, R8])
        gate_col = sb("gate_col", [P, NB])
        G = sb("G", [P, NB, R8])
        as_next = sb("as_next", [P, NCH, RANK])
        acc = ctx.enter_context(nc.psum_tensor("acc", [P, MB, 512], F32))
        cps = ctx.enter_context(nc.psum_tensor("cps", [P, 4, 512], F32))

        conv_out = cv_xq[:, 0:GR * NQ].rearrange("p (g q) -> p g q", g=GR)
        x_quads = cv_xq[:, GR * NQ:].rearrange("p (g q) -> p g q", g=GR)
        w_stage = [w_raw, b_mat]
        x_flat = x_raw[:].rearrange("p s w -> p (s w)")
        y_f32 = y_t[:].bitcast(F32)
        y_hi_out = y_t[:, :, 0, :].rearrange("p k (g o) -> p g k o", g=GR)
        y_lo_out = y_t[:, :, 1, :].rearrange("p k (g o) -> p g k o", g=GR)
        y_hi_in = y_f32[:, :, 0, :].rearrange("p k (g o) -> p g k o", g=GR)
        conv_ps = cps[:, 0:2, :].rearrange("p a (g q) -> p (a g) q", q=NQ)
        turn_ps = cps[:, 2:4, :].rearrange("p a (g k) -> p (a g) k", k=NQ)
        turned = turn_ps.rearrange("p g (k o) -> p g k o", o=GC)
        ax_ps = cps[:, 2, 0:2 * P]
        W_v = W.rearrange("(h c q s) m -> h c s q m", h=2, c=QC, s=S4)

        wpad = cv_xq[:, 0:15 * GC].rearrange("p (k i) -> p k i", i=GC)
        cwT4 = cv_xq[:, 480:992]
        condT = cv_xq[:, 992:1024]
        wraw = b_mat[:, 0:GC * TAPS].rearrange("p (i k) -> p k i", k=TAPS)
        cw_raw = b_mat[:, 288:416]
        cond_raw = b_mat[0:NS, 416:544]
        gate_exp = a_raw[0:NB, 0:2, :].rearrange("p a b -> p (a b)")
        stage_flat = stage[:].rearrange("p s l -> p (s l)")
        lora_A_raw = [stage_flat[:, k * HALF:(k + 1) * HALF] for k in range(RK)]
        As_raw = x_flat[0:RANK, 2 * XW:2 * XW + L]
        a_stage = x_flat[:, 2 * XW:2 * XW + L]
        a_mixed = acc[:].rearrange("p a n -> p (a n)")
        BR = 256
        lora_B_raw = b_mat[:, 0:2 * NL * RANK].rearrange("p (m n) -> p m n", m=2)
        lora_B_perm = w_raw[:, 0:1024].rearrange("p (k m n) -> p k m n", k=RK, m=2)
        b_turn = w_raw[:, 1024:2048]
        b_stage = w_raw[0:NB * R8, 0:RK * BR]
        b_ps = cps[:, 0:2, :].rearrange("p a n -> p (a n)")
        Bs_raw = b_mat[:, 1024:1536]
        Bs_out = b_mat[:, 1536:2048]

        conv_w_in = sem("conv_w_in")
        small_in = sem("small_in")
        la_raw_in = sem("la_raw_in")
        as_raw_in = sem("as_raw_in")
        id_ready = sem("id_ready")
        wpad_zero = sem("wpad_zero")
        wpad_ready = sem("wpad_ready")
        gexp_ready = sem("gexp_ready")
        rep_ready = sem("rep_ready")
        cwt_done = sem("cwt_done")
        ctxt_done = sem("ctxt_done")
        ctxt_ready = sem("ctxt_ready")
        gcol_done = sem("gcol_done")
        gcol_ready = sem("gcol_ready")
        ctx_done = sem("ctx_done")
        ctx_ready = sem("ctx_ready")
        g_ready = sem("g_ready")
        cw_hi_ready = sem("cw_hi_ready")
        cw_lo_ready = sem("cw_lo_ready")
        as_done = sem("as_done")
        as_copied = sem("as_copied")
        amix_done = sem("amix_done")
        amix_act = sem("amix_act")
        amix_dve = sem("amix_dve")
        amix_out = sem("amix_out")
        edge_zero = sem("edge_zero")
        lb_raw_in = sem("lb_raw_in")
        lb_perm = sem("lb_perm")
        bt_done = sem("bt_done")
        bt_ready = sem("bt_ready")
        bmix_done = sem("bmix_done")
        bmix_copied = sem("bmix_copied")
        bmix_out = sem("bmix_out")
        bs_raw_in = sem("bs_raw_in")
        bs_done = sem("bs_done")
        bs_copied = sem("bs_copied")
        bs_out = sem("bs_out")
        w_in = [sem("w_in0"), sem("w_in1")]
        w_hi_ready = sem("w_hi_ready")
        w_lo_ready = sem("w_lo_ready")
        w_chunk_used = sem("w_chunk_used")
        x_in = [sem(f"x_in{i}") for i in range(4)]
        xq_act = sem("xq_act")
        xq_dve = sem("xq_dve")
        x_hi_ready = sem("x_hi_ready")
        x_lo_ready = sem("x_lo_ready")
        conv_done = sem("conv_done")
        conv_copied = sem("conv_copied")
        turn_done = sem("turn_done")
        y_hi_ready = sem("y_hi_ready")
        y_lo_ready = sem("y_lo_ready")
        a_in = sem("a_in")
        as_switched = sem("as_switched")
        a_hi_ready = sem("a_hi_ready")
        a_lo_ready = sem("a_lo_ready")
        ax_done = sem("ax_done")
        ax_upper = sem("ax_upper")
        ax_sum = sem("ax_sum")
        ax_ready = sem("ax_ready")
        ax_stored = sem("ax_stored")
        axp_in = sem("axp_in")
        bs_in = sem("bs_in")
        b_in = sem("b_in")
        ffn_done = sem("ffn_done")
        out_dve = sem("out_dve")
        out_act = sem("out_act")
        stored = [sem("stored0"), sem("stored1")]
        part_in = [sem("part_in0"), sem("part_in1")]
        pre_added = sem("pre_added")

        def credit(eng, *sems_and_steps):
            for s, n in sems_and_steps:
                eng.sem_inc(s, n)

        def phases(eng, step):
            for ph in range(2):
                with eng.Fori(0, NB - 1) as i:
                    for j in range(SPB):
                        step(i, ph, j)
                for j in range(SPB):
                    step(NB - 1, ph, j)

        def load_x(eng, n, ph, slot):
            src = x[n][:, 0:XW] if ph == 0 else x[n][:, L - XW:L]
            eng.dma_start(x_raw[:, slot, :], src).then_inc(x_in[slot], 16)

        block = ctx.enter_context(nc.Block())

        @block.sync
        def _(sp):
            credit(sp, (stored[0], 16), (stored[1], 16), (ax_stored, 16), (bmix_out, 16))
            sp.dma_start(b_mat[:, 0:GC * TAPS], conv_w.rearrange("o i k -> o (i k)")).then_inc(conv_w_in, 16)
            load_x(sp, 0, 0, 0)
            sp.dma_start(gate_sb[:], gate).then_inc(small_in, 16)
            sp.dma_start(cw_raw, c_weight).then_inc(small_in, 16)
            sp.dma_start(cond_raw, cond).then_inc(small_in, 16)
            with nc.allow_non_contiguous_dma(reason="128 bias values, one per partition"):
                for s in range(S4):
                    sp.dma_start(bias_col[s * GC:(s + 1) * GC, :],
                                 conv_bias.rearrange("(g o) -> o g", g=GR)).then_inc(small_in, 16)

            def load_lora_A(ph):
                for k in range(RK):
                    sp.dma_start(lora_A_raw[k], lora_A[:, k * R8:(k + 1) * R8, ph * HALF:(ph + 1) * HALF]
                                 ).then_inc(la_raw_in, 16)

            load_lora_A(0)
            sp.dma_start(As_raw, lora_As).then_inc(as_raw_in, 16)
            load_x(sp, 1, 0, 1)
            for ph in range(2):
                sp.wait_ge(amix_act, ph + 1)
                sp.wait_ge(amix_dve, ph + 1)
                if ph == 0:
                    load_lora_A(1)
                sp.dma_start(mixed_A[ph].rearrange("p k n -> p (k n)"), a_stage).then_inc(amix_out, 16)
            sp.wait_ge(amix_out, 32)
            load_x(sp, 2, 0, 2)

            def step(i, ph, j):
                t = 32 * ph + 4 * i + j
                n = 4 * i + j
                last = type(i) is int
                if ph == 1 and not (last and j == 3):
                    sp.wait_ge(stored[(j + 1) % 2], 16 * (CREDIT + 16 * ph + 2 * i + (j + 1) // 2))
                sp.wait_ge(out_dve, CREDIT + t)
                if not (last and j >= 1):
                    load_x(sp, n + 3, ph, (j + 3) % 4)
                elif ph == 0:
                    load_x(sp, j - 1, 1, (j + 3) % 4)
                if ph == 0:
                    sp.wait_ge(ax_ready, CREDIT + t + 1)
                    sp.dma_start(partial_ax[n], ax[0:R2, :]).then_inc(ax_stored, 16)
                elif not (last and j == 3):
                    sp.wait_ge(ax_ready, CREDIT + t + 1)
                    sp.dma_start(ax_prev[:], partial_ax[n + 1]).then_inc(axp_in, 16)
                    sp.dma_start(stage[:, (j + 1) % 2, :], out[n + 1]).then_inc(part_in[(j + 1) % 2], 16)
                if ph == 1 and j == 0:
                    sp.dma_start(b_mat[0:RANK, :], mixed_B.rearrange("(b r) k m -> b (r k) m", b=NB)[i]).then_inc(b_in, 16)
                if ph == 0 and j == 0:
                    sp.wait_ge(w_lo_ready, NCH)
                    for m in range(2):
                        sp.dma_start(lora_B_raw[:, m, :].rearrange("p (n r) -> p n r", r=RANK),
                                     lora_B.rearrange("n (k m p) r -> k m p n r", m=2, p=P)[i, m]).then_inc(lb_raw_in, 16)
                    if last:
                        sp.dma_start(Bs_raw.rearrange("p (k r) -> p k r", r=RANK),
                                     lora_Bs.rearrange("(k p) r -> p k r", p=P)).then_inc(bs_raw_in, 16)
                if ph == 0 and j == 3:
                    sp.wait_ge(bmix_copied, i + 1)
                    sp.dma_start(mixed_B.rearrange("p k (i m) -> i p k m", m=BR)[i],
                                 b_stage.rearrange("p (k m) -> p k m", k=RK)).then_inc(bmix_out, 16)
                    if last:
                        sp.wait_ge(bs_copied, 1)
                        for k in range(4):
                            sp.dma_start(shared_B.rearrange("r (j k m) -> k r j m", k=4, m=P)[k],
                                         Bs_out[k * RANK:(k + 1) * RANK].rearrange("r (j m) -> r j m", m=P)
                                         ).then_inc(bs_out, 16)
                if j == 0 and not (last and ph == 1):
                    sp.wait_ge(a_lo_ready, 8 * ph + i + 1)
                    if last:
                        sp.dma_start(a_raw[:, :, 0:RANK], mixed_A[1, :, :, 0:RANK]).then_inc(a_in, 16)
                    else:
                        sp.dma_start(a_raw[:, :, 0:RANK],
                                     mixed_A[ph].rearrange("p k (b r) -> b p k r", r=RANK)[i + 1]).then_inc(a_in, 16)
                sp.wait_ge(out_dve, CREDIT + t + 1)
                if ph == 0:
                    sp.wait_ge(out_act, CREDIT + t + 1)
                sp.dma_start(out[n], stage[:, j % 2, :]).then_inc(stored[j % 2], 16)
                if ph == 0 and last and j == 3:
                    sp.wait_ge(stored[0], 16 * (CREDIT + 16))
                    sp.dma_start(stage[:, 0, :], out[0]).then_inc(part_in[0], 16)
                    sp.wait_ge(ax_stored, 16 * (CREDIT + NS))
                    sp.dma_start(ax_prev[:], partial_ax[0]).then_inc(axp_in, 16)
                    sp.wait_ge(w_lo_ready, 2 * NCH)
                    sp.wait_ge(bs_out, 64)
                    sp.wait_ge(bmix_out, 16 * (CREDIT + NB))
                    sp.dma_start(b_mat[RANK:R2, :], shared_B).then_inc(bs_in, 16)
                    sp.dma_start(b_mat[R2:R2 + 1, :], ffn_bias.rearrange("(a m) -> a m", a=1)).then_inc(bs_in, 16)

            phases(sp, step)
            sp.wait_ge(stored[0], 16 * (CREDIT + NS))
            sp.wait_ge(stored[1], 16 * (CREDIT + NS))

        @block.gpsimd
        def _(pool):
            nc.gpsimd.memset(ident[:], 0.0).then_inc(id_ready, 1)
            pool.wait_ge(id_ready, 1)
            nc.gpsimd.affine_select(out=ident[:], in_=ident[:], compare_op=ALU.not_equal, fill=1.0, base=0,
                                    pattern=[[-1, P]], channel_multiplier=1).then_inc(id_ready, 1)
            pool.wait_ge(id_ready, 2)
            nc.gpsimd.memset(ax[R2:R2 + 1, :], 1.0).then_inc(id_ready, 1)
            pool.wait_ge(id_ready, 3)

            def step(i, ph, j):
                t = 4 * i + j
                pool.wait_ge(x_in[j], 16 * (8 + i + 1))
                pool.wait_ge(part_in[j % 2], 16 * (2 * i + j // 2 + 1))
                nc.gpsimd.tensor_tensor(stage[:, j % 2, HALF:L], stage[:, j % 2, HALF:L],
                                        x_raw[:, j, PAD:XW], ALU.add).then_inc(pre_added, 1)

            with pool.Fori(0, NB) as i:
                for j in range(SPB):
                    step(i, 1, j)

        @block.scalar
        def _(act):
            credit(act, (out_act, 1))

            def load_w(k):
                if k >= 2:
                    act.wait_ge(w_lo_ready, k - 1)
                act.dma_start(w_stage[k % 2][:], W_v[k // NCH, k % NCH // S4, k % S4]).then_inc(w_in[k % 2], 16)

            def split_w(k):
                act.wait_ge(w_in[k % 2], 16 * (k // 2 + 1))
                if k == 2 * NCH - 1:
                    act.wait_ge(ffn_done, NS)
                elif k >= NCH:
                    act.wait_ge(w_chunk_used, k % NCH + 1)
                nc.scalar.copy(w_hi[:, k % NCH, :], w_stage[k % 2][:]).then_inc(w_hi_ready, 1)

            def x_rearrange(slot, in_value, t_plus_1, ph, first=False):
                act.wait_ge(x_in[slot], in_value)
                if not first:
                    act.wait_ge(x_lo_ready, t_plus_1 - 1)
                else:
                    act.wait_ge(edge_zero, 1)
                for g in range(2):
                    for r in range(S4):
                        ins = nc.scalar.copy(x_quads[r * GC:(r + 1) * GC, g, 1 - ph:1 - ph + NQ + 1],
                                             x_raw[g * GC:(g + 1) * GC, slot, r:XW:S4])
                ins.then_inc(xq_act, 1)

            def x_split(t_plus_1, first=False):
                act.wait_ge(xq_act, t_plus_1)
                act.wait_ge(xq_dve, t_plus_1)
                if not first:
                    act.wait_ge(conv_done, t_plus_1 - 1)
                nc.scalar.copy(x_hi[:], x_quads).then_inc(x_hi_ready, 1)

            def y_split(t_plus_1):
                act.wait_ge(turn_done, t_plus_1)
                nc.scalar.copy(y_hi_out, turned).then_inc(y_hi_ready, 1)

            def a_split(k_plus_1):
                act.wait_ge(a_in, 16 * k_plus_1)
                if type(k_plus_1) is int and k_plus_1 == NB + 1:
                    act.wait_ge(a_lo_ready, NB)
                    nc.scalar.copy(a_raw[:, :, RANK:R2], as_next[:]).then_inc(as_switched, 1)
                    act.wait_ge(as_switched, 1)
                nc.scalar.copy(a_parts[:, :, 0:R2], a_raw[:]).then_inc(a_hi_ready, 1)

            def a_mixed_copy(ph):
                act.wait_ge(amix_done, ph + 1)
                if ph == 0:
                    act.wait_ge(as_done, 1)
                else:
                    act.wait_ge(amix_out, 16)
                nc.scalar.copy(a_stage[:, 0:HALF], a_mixed[:, 0:HALF]).then_inc(amix_act, 1)

            x_rearrange(0, 16, 1, 0, first=True)
            act.wait_ge(cwt_done, 1)
            for d in range(3):
                ins = nc.scalar.copy(cw_hi[:, d].rearrange("p g (s o) -> p s g o", s=S4),
                                     cps[:, d, :].rearrange("p (s g o) -> p s g o", s=S4, g=GR))
            ins.then_inc(cw_hi_ready, 1)
            x_split(1, first=True)
            load_w(0)
            act.wait_ge(ctxt_done, 1)
            load_w(1)
            a_mixed_copy(0)
            x_rearrange(1, 16, 2, 0)
            x_split(2)
            a_split(1)
            y_split(1)
            split_w(0)
            load_w(2)
            a_mixed_copy(1)
            for k in range(1, NCH):
                split_w(k)
                if k + 2 < NCH:
                    load_w(k + 2)

            def step(i, ph, j):
                t = 32 * ph + 4 * i + j
                last = type(i) is int
                act.wait_ge(ax_done, t + 1)
                act.wait_ge(ax_ready, CREDIT + t)
                nc.scalar.copy(ax_tmp[:], ax_ps[R2:P, :]).then_inc(ax_upper, 1)
                more = not (ph == 1 and last)
                if ph == 0 and j == 1:
                    act.wait_ge(lb_raw_in, 32 * i + 32)
                    act.wait_ge(bmix_out, 16 * (CREDIT + i))
                    for m in range(2):
                        nc.scalar.copy(lora_B_perm[:, :, m, :].rearrange("p k (n r) -> p k n r", r=R8),
                                       lora_B_raw[:, m, :].rearrange("p (n k r) -> p k n r", k=RK, r=R8)
                                       ).then_inc(lb_perm, 1)
                if more or j < 2:
                    nph = 1 if last and j >= 2 else ph
                    x_rearrange((j + 2) % 4, 16 * (8 * ph + i + (j + 2) // 4 + 1), t + 3, nph)
                    x_split(t + 3)
                if j == 3 and more:
                    a_split(8 * ph + i + 2)
                if ph == 0 and j == 1:
                    act.wait_ge(bt_done, i + 1)
                    nc.scalar.copy(b_turn, b_ps).then_inc(bt_ready, 1)
                if ph == 0 and last and j == 2:
                    act.wait_ge(bs_done, 1)
                    nc.scalar.copy(Bs_out, cps[:, 3, :]).then_inc(bs_copied, 1)
                if ph == 0 and last and j == 3:
                    act.wait_ge(bmix_out, 16 * (CREDIT + NB))
                    act.wait_ge(bs_out, 64)
                    load_w(NCH)
                    load_w(NCH + 1)
                    for k in range(NCH, NCH + W_EARLY):
                        split_w(k)
                        load_w(k + 2)
                if ph == 0:
                    act.wait_ge(ffn_done, t + 1)
                    act.wait_ge(stored[j % 2], 16 * (CREDIT + 2 * i + j // 2))
                    nc.scalar.copy(stage[:, j % 2, HALF:L], acc[:, 2:4, :].rearrange("p a n -> p (a n)")
                                   ).then_inc(out_act, 1)
                if more or j < 3:
                    y_split(t + 2)
                if ph == 0 and last and j == 3:
                    for k in range(NCH + W_EARLY, 2 * NCH):
                        split_w(k)
                        if k + 2 < 2 * NCH:
                            load_w(k + 2)

            phases(act, step)

        @block.vector
        def _(dve):
            credit(dve, (out_dve, 1), (ax_ready, 1))
            V = nc.vector

            def split_w(k):
                dve.wait_ge(w_hi_ready, k + 1)
                V.tensor_tensor(w_lo[:, k % NCH, :], w_stage[k % 2][:], w_hi[:, k % NCH, :].bitcast(F32),
                                ALU.subtract).then_inc(w_lo_ready, 1)

            def x_rearrange(slot, in_value, t_plus_1, ph, first=False):
                dve.wait_ge(x_in[slot], in_value)
                if not first:
                    dve.wait_ge(x_hi_ready, t_plus_1 - 1)
                    dve.wait_ge(x_lo_ready, t_plus_1 - 1)
                for g in range(2, GR):
                    for r in range(S4):
                        ins = V.tensor_copy(x_quads[r * GC:(r + 1) * GC, g, 1 - ph:1 - ph + NQ + 1],
                                            x_raw[g * GC:(g + 1) * GC, slot, r:XW:S4])
                ins.then_inc(xq_dve, 1)

            def x_split(t_plus_1):
                dve.wait_ge(xq_dve, t_plus_1)
                dve.wait_ge(x_hi_ready, t_plus_1)
                V.tensor_tensor(x_lo[:], x_quads, x_hi[:].bitcast(F32), ALU.subtract).then_inc(x_lo_ready, 1)

            def conv_copy(n, t_plus_1):
                dve.wait_ge(conv_done, t_plus_1)
                bias = ctx_bias[:, n, :].unsqueeze(2).to_broadcast([P, GR, NQ])
                V.tensor_tensor(conv_out, conv_ps, bias, ALU.add).then_inc(conv_copied, 1)

            def y_split(t_plus_1):
                dve.wait_ge(y_hi_ready, t_plus_1)
                V.tensor_tensor(y_lo_out, turned, y_hi_in, ALU.subtract).then_inc(y_lo_ready, 1)

            def a_split(k_plus_1):
                dve.wait_ge(a_hi_ready, k_plus_1)
                V.tensor_tensor(a_parts[:, :, R2:2 * R2], a_raw[:], a_parts[:, :, 0:R2].bitcast(F32),
                                ALU.subtract).then_inc(a_lo_ready, 1)

            V.memset(wpad, 0.0).then_inc(wpad_zero, 1)
            V.memset(x_quads[:, :, 0:1], 0.0).then_inc(edge_zero, 1)
            dve.wait_ge(conv_w_in, 16)
            dve.wait_ge(wpad_zero, 1)
            V.tensor_copy(wpad[:, 3:3 + TAPS, :], wraw).then_inc(wpad_ready, 1)
            dve.wait_ge(id_ready, 2)
            V.tensor_reduce(rep[:], ident[:].rearrange("p (a r) -> p r a", r=R8), AX_X, ALU.add).then_inc(rep_ready, 1)
            x_rearrange(0, 16, 1, 0, first=True)
            dve.wait_ge(small_in, 16 * 7)
            V.tensor_copy(gate_exp.rearrange("b (n r) -> b n r", r=R8),
                          gate_sb[:].unsqueeze(2).to_broadcast([NB, NL, R8])).then_inc(gexp_ready, 1)
            dve.wait_ge(ctxt_done, 1)
            V.tensor_copy(cwT4.rearrange("p (g s o) -> p g s o", g=GR, s=S4),
                          acc[:, 0, 0:CH].rearrange("p (g o) -> p g o", g=GR).unsqueeze(2).to_broadcast([P, GR, S4, GC])
                          ).then_inc(ctxt_ready, 1)
            V.tensor_copy(condT, acc[:, 0, CH:CH + NS]).then_inc(ctxt_ready, 1)
            dve.wait_ge(gcol_done, 1)
            V.tensor_copy(gate_col[:], acc[:, 1, 0:NB]).then_inc(gcol_ready, 1)
            dve.wait_ge(gcol_ready, 1)
            dve.wait_ge(rep_ready, 1)
            V.tensor_tensor(G[:], gate_col[:].unsqueeze(2).to_broadcast([P, NB, R8]),
                            rep[:].unsqueeze(1).to_broadcast([P, NB, R8]), ALU.mult).then_inc(g_ready, 1)
            dve.wait_ge(cw_hi_ready, 1)
            for d in range(3):
                ins = V.tensor_tensor(cw_lo[:, d].rearrange("p g (s o) -> p s g o", s=S4),
                                      cps[:, d, :].rearrange("p (s g o) -> p s g o", s=S4, g=GR),
                                      cw_hi[:, d].bitcast(F32).rearrange("p g (s o) -> p s g o", s=S4), ALU.subtract)
            ins.then_inc(cw_lo_ready, 1)
            dve.wait_ge(edge_zero, 1)
            x_split(1)
            dve.wait_ge(ctx_done, 1)
            V.tensor_tensor(ctx_bias[:].rearrange("p n g -> p g n"),
                            acc[:, 2, 0:P].rearrange("p (g n) -> p g n", g=GR),
                            bias_col[:].unsqueeze(2).to_broadcast([P, GR, NS]), ALU.add).then_inc(ctx_ready, 1)
            dve.wait_ge(as_done, 1)
            V.tensor_copy(a_raw[:, :, RANK:R2], cps[:, 3, 0:NCH * RANK].rearrange("p (k r) -> p k r", r=RANK)
                          ).then_inc(as_copied, 1)
            V.tensor_copy(as_next[:], cps[:, 3, NCH * RANK:2 * NCH * RANK].rearrange("p (k r) -> p k r", r=RANK)
                          ).then_inc(as_copied, 1)

            def a_mixed_copy(ph):
                dve.wait_ge(amix_done, ph + 1)
                if ph == 1:
                    dve.wait_ge(amix_out, 16)
                V.tensor_copy(a_stage[:, HALF:L], a_mixed[:, HALF:L]).then_inc(amix_dve, 1)

            a_mixed_copy(0)
            dve.wait_ge(amix_act, 1)
            V.tensor_copy(a_raw[:, :, 0:RANK], a_mixed.rearrange("p (k n) -> p k n", k=NCH)[:, :, 0:RANK]).then_inc(a_in, 16)
            dve.wait_ge(ctx_ready, 1)
            conv_copy(0, 1)
            x_rearrange(1, 16, 2, 0)
            x_split(2)
            a_split(1)
            y_split(1)
            split_w(0)
            a_mixed_copy(1)
            for k in range(1, NCH):
                split_w(k)

            def step(i, ph, j):
                t = 32 * ph + 4 * i + j
                n = 4 * i + j
                last = type(i) is int
                more = not (ph == 1 and last)
                if more or j < 3:
                    conv_copy((n + 1) if not (last and j == 3) else 0, t + 2)
                dve.wait_ge(ax_upper, t + 1)
                V.tensor_tensor(ax_tmp[:], ax_ps[0:R2, :], ax_tmp[:], ALU.add).then_inc(ax_sum, 1)
                dve.wait_ge(ax_sum, t + 1 if ph == 0 else NS + 2 * n + 1)
                if ph == 0:
                    dve.wait_ge(ax_stored, 16 * (CREDIT + t))
                    V.tensor_tensor(ax[0:R2, :], ax_tmp[:, 0:P], ax_tmp[:, P:2 * P], ALU.add).then_inc(ax_ready, 1)
                else:
                    V.tensor_tensor(ax_tmp[:, 0:P], ax_tmp[:, 0:P], ax_tmp[:, P:2 * P], ALU.add).then_inc(ax_sum, 1)
                    dve.wait_ge(axp_in, 16 * (4 * i + j + 1))
                    dve.wait_ge(ax_stored, 16 * (CREDIT + NS))
                    dve.wait_ge(ax_sum, NS + 2 * (4 * i + j) + 2)
                    V.tensor_tensor(ax[0:R2, :], ax_tmp[:, 0:P], ax_prev[:], ALU.add).then_inc(ax_ready, 1)
                if more or j < 2:
                    nph = 1 if last and j >= 2 else ph
                    if ph == 0 and last and j == 2:
                        dve.wait_ge(x_hi_ready, t + 2)
                        dve.wait_ge(x_lo_ready, t + 2)
                        V.memset(x_quads[:, :, XQ - 1:XQ], 0.0).then_inc(edge_zero, 1)
                    x_rearrange((j + 2) % 4, 16 * (8 * ph + i + (j + 2) // 4 + 1), t + 3, nph)
                    if ph == 0 and last and j == 2:
                        dve.wait_ge(edge_zero, 2)
                    x_split(t + 3)
                if j == 3 and more:
                    a_split(8 * ph + i + 2)
                if ph == 0 and last and j == 3:
                    for k in range(NCH, NCH + W_EARLY):
                        split_w(k)
                if ph == 0 and j == 2:
                    dve.wait_ge(bmix_done, i + 1)
                    V.tensor_copy(b_stage, b_ps[0:NB * R8, :]).then_inc(bmix_copied, 1)
                dve.wait_ge(ffn_done, t + 1)
                if ph == 0:
                    dve.wait_ge(stored[j % 2], 16 * (CREDIT + 2 * i + j // 2))
                    V.tensor_tensor(stage[:, j % 2, 0:HALF], acc[:, 0:2, :].rearrange("p a n -> p (a n)"),
                                    x_raw[:, j, 0:HALF], ALU.add).then_inc(out_dve, 1)
                else:
                    dve.wait_ge(pre_added, 4 * i + j + 1)
                    V.tensor_tensor(stage[:, j % 2, :], acc[:].rearrange("p a n -> p (a n)"), stage[:, j % 2, :],
                                    ALU.add).then_inc(out_dve, 1)
                if more or j < 3:
                    y_split(t + 2)
                if ph == 0 and last and j == 3:
                    for k in range(NCH + W_EARLY, 2 * NCH):
                        split_w(k)

            phases(dve, step)

        @block.tensor
        def _(pe):
            T = nc.tensor

            def conv(t_plus_1):
                pe.wait_ge(x_lo_ready, t_plus_1)
                for g in range(GR):
                    n = 0
                    for d in range(3):
                        for wt, xt in ((cw_hi, x_hi), (cw_hi, x_lo), (cw_lo, x_hi)):
                            ins = T.matmul(conv_ps[:, g, :], wt[:, d, g, :], xt[:, g, d:d + NQ],
                                           start=(n == 0), stop=(n == 8))
                            n += 1
                ins.then_inc(conv_done, 1)

            def turn(t_plus_1):
                pe.wait_ge(conv_copied, t_plus_1)
                for g in range(GR):
                    for c in range(QC):
                        ins = T.transpose(turn_ps[:, g, c * P:(c + 1) * P], conv_out[:, g, c * P:(c + 1) * P],
                                          ident[:])
                ins.then_inc(turn_done, 1)

            pe.wait_ge(id_ready, 3)
            pe.wait_ge(wpad_ready, 1)
            wp = wpad.rearrange("p k i -> p (k i)")
            for d in range(3):
                for s in range(S4):
                    k0 = (4 * d + 3 - s) * GC
                    ins = T.transpose(cps[:, d, s * P:(s + 1) * P], wp[:, k0:k0 + P], ident[:])
            ins.then_inc(cwt_done, 1)
            pe.wait_ge(small_in, 16 * 7)
            T.transpose(acc[:, 0, 0:CH], cw_raw, ident[:])
            T.transpose(acc[:, 0, CH:CH + NS], cond_raw, ident[0:NS, 0:NS]).then_inc(ctxt_done, 1)
            pe.wait_ge(gexp_ready, 1)
            T.matmul(acc[:, 1, 0:NB], gate_exp, ident[0:NB, 0:NB], start=True, stop=True).then_inc(gcol_done, 1)
            pe.wait_ge(ctxt_ready, 2)
            for g in range(GR):
                ins = T.matmul(acc[:, 2, g * NS:(g + 1) * NS], cwT4[:, g * P:(g + 1) * P], condT, start=True, stop=True)
            ins.then_inc(ctx_done, 1)
            pe.wait_ge(cw_lo_ready, 1)
            conv(1)
            pe.wait_ge(as_raw_in, 16)
            for ch in range(2 * NCH):
                l0 = ch // S4 * 512 + ch % S4
                ins = T.transpose(cps[:, 3, ch * RANK:(ch + 1) * RANK], As_raw[:, l0:l0 + 509:S4], ident[0:RANK, 0:RANK])
            ins.then_inc(as_done, 1)

            def mix_A(ph):
                pe.wait_ge(la_raw_in, 16 * RK * (ph + 1))
                for ch in range(NCH):
                    l0 = ch // S4 * 512 + ch % S4
                    dst = a_mixed[:, ch * 256:(ch + 1) * 256].rearrange("p (b r k) -> p k b r", r=R8, k=RK)
                    for k in range(RK):
                        ins = T.matmul(dst[:, k], lora_A_raw[k][:, l0:l0 + 509:S4], G[:].rearrange("p b r -> p (b r)"),
                                       start=True, stop=True)
                ins.then_inc(amix_done, 1)

            pe.wait_ge(g_ready, 1)
            pe.wait_ge(ctx_ready, 1)
            mix_A(0)
            pe.wait_ge(as_copied, 2)
            turn(1)
            conv(2)
            pe.wait_ge(a_in, 16)
            mix_A(1)
            pe.wait_ge(amix_act, 2)
            pe.wait_ge(amix_dve, 2)

            def mix_B(i, j, last):
                if j == 1:
                    pe.wait_ge(lb_perm, 2 * i + 2)
                    pe.wait_ge(conv_copied, 4 * i + j + 2)
                    for k in range(RK):
                        for m in range(2):
                            ins = T.transpose(b_ps[:, k * BR + m * P:k * BR + (m + 1) * P], lora_B_perm[:, k, m, :],
                                              ident[:])
                    ins.then_inc(bt_done, 1)
                if j == 2:
                    pe.wait_ge(bt_ready, i + 1)
                    pe.wait_ge(conv_copied, 4 * i + j + 2)
                    for k in range(RK):
                        ins = T.matmul(b_ps[0:NB * R8, k * BR:(k + 1) * BR], G[:].rearrange("p b r -> p (b r)"),
                                       b_turn[:, k * BR:(k + 1) * BR], start=True, stop=True)
                    ins.then_inc(bmix_done, 1)
                    if last:
                        pe.wait_ge(bs_raw_in, 16)
                        for k in range(4):
                            ins = T.transpose(cps[:, 3, k * P:(k + 1) * P], Bs_raw[:, k * P:(k + 1) * P], ident[:])
                        ins.then_inc(bs_done, 1)

            def step(i, ph, j):
                t = 32 * ph + 4 * i + j
                last = type(i) is int
                more = not (ph == 1 and last)
                if j == 0:
                    pe.wait_ge(a_lo_ready, 8 * ph + i + 1)
                pe.wait_ge(y_lo_ready, t + 1)
                for ch in range(NCH):
                    ins = T.matmul(ax_ps, a_parts[:, ch, :], y_t[:, ch].rearrange("p h r -> p (h r)"),
                                   start=(ch == 0), stop=(ch == NCH - 1))
                ins.then_inc(ax_done, 1)
                pe.wait_ge(out_dve, CREDIT + t)
                if ph == 0:
                    pe.wait_ge(out_act, CREDIT + t)
                elif j == 0:
                    pe.wait_ge(out_act, CREDIT + NS)
                for ch in range(NCH):
                    if j == 0:
                        pe.wait_ge(w_lo_ready, NCH * ph + ch + 1)
                    for part, wt in ((0, w_hi), (0, w_lo), (1, w_hi)):
                        for m in range(MB):
                            ins = T.matmul(acc[:, m, :], y_t[:, ch, part, :], wt[:, ch, m * 512:(m + 1) * 512],
                                           start=(ch == 0 and part == 0 and wt is w_hi),
                                           stop=(ph == 0 and ch == NCH - 1 and part == 1))
                    if ph == 0 and ch == NCH // 2:
                        mix_B(i, j, last)
                    if ph == 0 and last and j == 3:
                        if ch < NCH - 1:
                            ins.then_inc(w_chunk_used, 1)
                if ph == 0:
                    ins.then_inc(ffn_done, 1)
                else:
                    pe.wait_ge(ax_ready, CREDIT + t + 1)
                    if j == 0:
                        pe.wait_ge(bs_in, 32)
                        pe.wait_ge(b_in, 16 * (i + 1))
                    for m in range(MB):
                        ins = T.matmul(acc[:, m, :], ax[0:R2 + 1, :], b_mat[0:R2 + 1, m * 512:(m + 1) * 512],
                                       start=False, stop=True)
                    ins.then_inc(ffn_done, 1)
                if more or j < 3:
                    pe.wait_ge(ax_ready, CREDIT + t + 1)
                    if ph == 0 and last and j == 2:
                        pe.wait_ge(bs_copied, 1)
                    turn(t + 2)
                if more or j < 2:
                    if ph == 0 and j == 1:
                        pe.wait_ge(bt_ready, i + 1)
                    if ph == 0 and j == 2:
                        pe.wait_ge(bmix_copied, i + 1)
                    conv(t + 3)

            phases(pe, step)


INPUTS = ["x", "cond_128", "fside_S_0", "L0_cond_weight", "L0_cond_c_weight", "L0_ffn_gate", "L0_ffn_kernel",
          "L0_ffn_bias", "L0_ffn_lora_A", "L0_ffn_lora_B", "L0_ffn_lora_A_shared", "L0_ffn_lora_B_shared"]


def kernel(**inputs):
    import numpy as np
    import concourse.bacc as bacc
    from concourse.bass_utils import run_bass_kernel_spmd

    nc = bacc.Bacc("TRN2", target_bir_lowering=False, num_devices=1, dynamic_dma_scratch_size=1024)
    arrays, aps = {}, []
    for name in INPUTS:
        a = np.ascontiguousarray(inputs[name])
        arrays[f"in_{name}"] = a
        aps.append(nc.dram_tensor(f"in_{name}", a.shape, mybir.dt.from_np(a.dtype), kind="ExternalInput").ap())
    out = nc.dram_tensor("out", (NS, CH, L), F32, kind="ExternalOutput").ap()
    build(nc, *aps, out)
    r = run_bass_kernel_spmd(nc, [arrays], core_ids=[0])
    return r.results[0]["out"]
```

```python
from contextlib import ExitStack

import concourse.bass as bass
from concourse import mybir

F32 = mybir.dt.float32
F32R = mybir.dt.float32r
ALU = mybir.AluOpType
AX_X = mybir.AxisListType.X

P = 128
NS, CH, L = 32, 128, 2048
GR, TAPS, PAD = 4, 9, 4
GC = CH // GR
S4 = 4
HALF = L // 2
NQ = HALF // S4
QC = NQ // P
NCH = HALF // P
XW = HALF + PAD
XQ = NQ + 2
MB = L // 512
NB, RANK, NL = 8, 32, 16
SPB = NS // NB
R2 = 2 * RANK
W_EARLY = 5
R8 = P // NL
RK = RANK // R8
CREDIT = 1


def build(nc, x, cond, conv_bias, conv_w, c_weight, gate, W, ffn_bias, lora_A, lora_B, lora_As, lora_Bs, out):
    mixed_A = nc.dram_tensor("mixed_A", (2, P, NCH, NB * RANK), F32, kind="Internal").ap()
    mixed_B = nc.dram_tensor("mixed_B", (NB * R8, RK, L), F32, kind="Internal").ap()
    shared_B = nc.dram_tensor("shared_B", (RANK, L), F32, kind="Internal").ap()
    partial_ax = nc.dram_tensor("partial_ax", (NS, P, P), F32, kind="Internal").ap()

    with ExitStack() as ctx:
        def sb(name, shape, dt=F32):
            return ctx.enter_context(nc.sbuf_tensor(name, shape, dt))

        def sem(name):
            return ctx.enter_context(nc.semaphore(name))

        w_hi = sb("w_hi", [P, NCH, L], F32R)
        w_lo = sb("w_lo", [P, NCH, L], F32R)
        y_t = sb("y_t", [P, NCH, 2, P], F32R)
        stage = sb("stage", [P, L])
        x_raw = sb("x_raw", [P, 4, XW])
        cv_xq = sb("cv_xq", [P, GR * NQ + GR * XQ])
        x_hi = sb("x_hi", [P, GR, XQ], F32R)
        x_lo = sb("x_lo", [P, GR, XQ], F32R)
        cw_hi = sb("cw_hi", [P, 3, GR, P], F32R)
        cw_lo = sb("cw_lo", [P, 3, GR, P], F32R)
        b_parts = sb("b_parts", [P, L], F32R)
        w_raw = sb("w_raw", [P, L])
        bias_half = sb("bias_half", [P, HALF])
        a_raw = sb("a_raw", [P, NCH, R2])
        a_parts = sb("a_parts", [P, NCH, 2 * R2], F32R)
        ident = sb("ident", [P, P])
        ax_tmp = sb("ax_tmp", [P, 2 * P])
        ax = sb("ax", [P, P])
        ax_prev = sb("ax_prev", [P, P])
        ax_hi = sb("ax_hi", [P, P], F32R)
        ax_lo = sb("ax_lo", [P, P], F32R)
        ctx_bias = sb("ctx_bias", [P, NS, GR])
        bias_col = sb("bias_col", [P, GR])
        gate_sb = sb("gate_sb", [NB, NL])
        rep = sb("rep", [P, R8])
        gate_col = sb("gate_col", [P, NB])
        G = sb("G", [P, NB, R8])
        as_next = sb("as_next", [P, NCH, RANK])
        acc = ctx.enter_context(nc.psum_tensor("acc", [P, MB, 512], F32))
        cps = ctx.enter_context(nc.psum_tensor("cps", [P, 4, 512], F32))

        conv_out = cv_xq[:, 0:GR * NQ].rearrange("p (g q) -> p g q", g=GR)
        x_quads = cv_xq[:, GR * NQ:].rearrange("p (g q) -> p g q", g=GR)
        WP = L // 4
        w_stage = [w_raw[:, k * WP:(k + 1) * WP] for k in range(4)]
        x_flat = x_raw[:].rearrange("p s w -> p (s w)")
        y_f32 = y_t[:].bitcast(F32)
        y_hi_out = y_t[:, :, 0, :].rearrange("p k (g o) -> p g k o", g=GR)
        y_lo_out = y_t[:, :, 1, :].rearrange("p k (g o) -> p g k o", g=GR)
        y_hi_in = y_f32[:, :, 0, :].rearrange("p k (g o) -> p g k o", g=GR)
        conv_ps = cps[:, 0:2, :].rearrange("p a (g q) -> p (a g) q", q=NQ)
        turn_ps = cps[:, 2:4, :].rearrange("p a (g k) -> p (a g) k", k=NQ)
        turned = turn_ps.rearrange("p g (k o) -> p g k o", o=GC)
        ax_ps = cps[:, 2, 0:2 * P]
        W_v = W.rearrange("(h c q s) (w m) -> h c s w q m", h=2, c=QC, s=S4, m=WP)

        wpad = cv_xq[:, 0:15 * GC].rearrange("p (k i) -> p k i", i=GC)
        cwT4 = cv_xq[:, 480:992]
        condT = cv_xq[:, 992:1024]
        wraw = bias_half[:, 0:GC * TAPS].rearrange("p (i k) -> p k i", k=TAPS)
        cw_raw = bias_half[:, 288:416]
        cond_raw = bias_half[0:NS, 416:544]
        gate_exp = a_raw[0:NB, 0:2, :].rearrange("p a b -> p (a b)")
        lora_A_raw = [stage[:, k * HALF:(k + 1) * HALF] for k in range(2)]
        As_raw = x_flat[0:RANK, 2 * XW:2 * XW + L]
        a_stage = x_flat[:, 2 * XW:2 * XW + L]
        a_mixed = acc[:].rearrange("p a n -> p (a n)")
        lora_B_raw = w_raw[:, 0:512]
        lora_B_perm = w_raw[:, 512:1024].rearrange("p (k n) -> p k n", k=RK)
        b_turn = w_raw[:, 1024:1536]
        b_stage = w_raw[0:NB * R8, 1536:2048]
        Bs_raw = w_raw[:, 0:512]
        Bs_out = w_raw[:, 1536:2048]

        conv_w_in = sem("conv_w_in")
        small_in = sem("small_in")
        la_raw_in = [sem("la_raw_in0"), sem("la_raw_in1")]
        la_block_used = sem("la_block_used")
        as_raw_in = sem("as_raw_in")
        id_ready = sem("id_ready")
        wpad_zero = sem("wpad_zero")
        wpad_ready = sem("wpad_ready")
        gexp_ready = sem("gexp_ready")
        rep_ready = sem("rep_ready")
        cwt_done = sem("cwt_done")
        ctxt_done = sem("ctxt_done")
        ctxt_ready = sem("ctxt_ready")
        gcol_done = sem("gcol_done")
        gcol_ready = sem("gcol_ready")
        ctx_done = sem("ctx_done")
        ctx_ready = sem("ctx_ready")
        g_ready = sem("g_ready")
        cw_hi_ready = sem("cw_hi_ready")
        cw_lo_ready = sem("cw_lo_ready")
        as_done = sem("as_done")
        as_copied = sem("as_copied")
        amix_act = sem("amix_act")
        amix_dve = sem("amix_dve")
        amix_out = sem("amix_out")
        edge_zero = sem("edge_zero")
        lb_raw_in = sem("lb_raw_in")
        lb_perm = sem("lb_perm")
        bt_done = sem("bt_done")
        bt_ready = sem("bt_ready")
        bmix_done = sem("bmix_done")
        bmix_copied = sem("bmix_copied")
        bmix_out = sem("bmix_out")
        bs_raw_in = sem("bs_raw_in")
        bs_done = sem("bs_done")
        bs_copied = sem("bs_copied")
        bs_out = sem("bs_out")
        w_in = [sem(f"w_in{k}") for k in range(4)]
        w_hi_ready = sem("w_hi_ready")
        w_lo_ready = sem("w_lo_ready")
        w_chunk_used = sem("w_chunk_used")
        x_in = [sem(f"x_in{i}") for i in range(4)]
        xq_act = sem("xq_act")
        xq_dve = sem("xq_dve")
        x_hi_ready = sem("x_hi_ready")
        x_lo_ready = sem("x_lo_ready")
        conv_done = sem("conv_done")
        conv_copied = sem("conv_copied")
        turn_done = sem("turn_done")
        y_hi_ready = sem("y_hi_ready")
        y_lo_ready = sem("y_lo_ready")
        a_in = sem("a_in")
        as_switched = sem("as_switched")
        a_hi_ready = sem("a_hi_ready")
        a_lo_ready = sem("a_lo_ready")
        ax_done = sem("ax_done")
        ax_upper = sem("ax_upper")
        ax_sum = sem("ax_sum")
        ax_ready = sem("ax_ready")
        ax_hi_ready = sem("ax_hi_ready")
        ax_lo_ready = sem("ax_lo_ready")
        ax_stored = sem("ax_stored")
        axp_in = sem("axp_in")
        bs_in = sem("bs_in")
        b_in = sem("b_in")
        b_hi_ready = sem("b_hi_ready")
        b_lo_ready = sem("b_lo_ready")
        ffn_done = sem("ffn_done")
        out_copied = sem("out_copied")
        bias_in = sem("bias_in")
        stored = sem("stored")
        part_in = sem("part_in")
        pre_added = sem("pre_added")

        def credit(eng, *sems_and_steps):
            for s, n in sems_and_steps:
                eng.sem_inc(s, n)

        def phases(eng, step):
            for ph in range(2):
                with eng.Fori(0, NB - 1) as i:
                    for j in range(SPB):
                        step(i, ph, j)
                for j in range(SPB):
                    step(NB - 1, ph, j)

        def load_x(eng, n, ph, slot):
            src = x[n][:, 0:XW] if ph == 0 else x[n][:, L - XW:L]
            eng.dma_start(x_raw[:, slot, :], src).then_inc(x_in[slot], 16)

        block = ctx.enter_context(nc.Block())

        @block.sync
        def _(sp):
            credit(sp, (stored, 16), (ax_stored, 16), (bmix_out, 16))
            sp.dma_start(bias_half[:, 0:GC * TAPS], conv_w.rearrange("o i k -> o (i k)")).then_inc(conv_w_in, 16)
            load_x(sp, 0, 0, 0)
            sp.dma_start(gate_sb[:], gate).then_inc(small_in, 16)
            sp.dma_start(cw_raw, c_weight).then_inc(small_in, 16)
            sp.dma_start(cond_raw, cond).then_inc(small_in, 16)
            with nc.allow_non_contiguous_dma(reason="128 bias values, one per partition"):
                for s in range(S4):
                    sp.dma_start(bias_col[s * GC:(s + 1) * GC, :],
                                 conv_bias.rearrange("(g o) -> o g", g=GR)).then_inc(small_in, 16)

            def load_lora_A(k):
                if k >= 2:
                    sp.wait_ge(la_block_used, k - 1)
                ph, r = k // RK, k % RK
                sp.dma_start(lora_A_raw[k % 2], lora_A[:, r * R8:(r + 1) * R8, ph * HALF:(ph + 1) * HALF]
                             ).then_inc(la_raw_in[k % 2], 16)

            def load_bias(ph):
                half = slice(HALF, L) if ph == 0 else slice(0, HALF)
                sp.dma_start(bias_half[:], ffn_bias.rearrange("(a m) -> a m", a=1)[:, half].to_broadcast([P, HALF])
                             ).then_inc(bias_in, 16)

            load_lora_A(0)
            load_lora_A(1)
            sp.dma_start(As_raw, lora_As).then_inc(as_raw_in, 16)
            load_x(sp, 1, 0, 1)
            for k in range(2, 6):
                load_lora_A(k)
            for ph in range(2):
                sp.wait_ge(amix_act, ph + 1)
                sp.wait_ge(amix_dve, ph + 1)
                sp.dma_start(mixed_A[ph].rearrange("p k n -> p (k n)"), a_stage).then_inc(amix_out, 16)
                if ph == 0:
                    load_lora_A(6)
                    load_lora_A(7)
            sp.wait_ge(ctxt_done, 1)
            load_bias(0)
            sp.wait_ge(amix_out, 32)
            load_x(sp, 2, 0, 2)

            def step(i, ph, j):
                t = 32 * ph + 4 * i + j
                n = 4 * i + j
                last = type(i) is int
                if ph == 1:
                    sp.wait_ge(stored, 16 * (CREDIT + t))
                sp.wait_ge(out_copied, CREDIT + t)
                if not (last and j >= 1):
                    load_x(sp, n + 3, ph, (j + 3) % 4)
                elif ph == 0:
                    load_x(sp, j - 1, 1, (j + 3) % 4)
                if ph == 1:
                    sp.dma_start(stage[:], out[n]).then_inc(part_in, 16)
                if ph == 1 and j == 0:
                    for rows in (0, R2):
                        sp.dma_start(w_raw[rows:rows + RANK, :], mixed_B.rearrange("(b r) k m -> b (r k) m", b=NB)[i]
                                     ).then_inc(b_in, 16)
                if ph == 0 and j in (1, 2):
                    if j == 1:
                        sp.wait_ge(w_lo_ready, 4 * NCH)
                    if last and j == 1:
                        sp.wait_ge(bs_done, 1)
                    sp.dma_start(lora_B_raw.rearrange("p (n r) -> p n r", r=RANK),
                                 lora_B.rearrange("n (q p) r -> q p n r", p=P)[2 * i + j - 1]).then_inc(lb_raw_in, 16)
                if ph == 0 and last and j == 0:
                    sp.dma_start(Bs_raw.rearrange("p (k r) -> p k r", r=RANK),
                                 lora_Bs.rearrange("(k p) r -> p k r", p=P)).then_inc(bs_raw_in, 16)
                sp.wait_ge(ax_ready, CREDIT + t + 1)
                if ph == 0:
                    sp.dma_start(partial_ax[n], ax[:]).then_inc(ax_stored, 16)
                elif not (last and j == 3):
                    sp.dma_start(ax_prev[:], partial_ax[n + 1]).then_inc(axp_in, 16)
                if j == 0 and not (last and ph == 1):
                    sp.wait_ge(a_lo_ready, 8 * ph + i + 1)
                    if last:
                        sp.dma_start(a_raw[:, :, 0:RANK], mixed_A[1, :, :, 0:RANK]).then_inc(a_in, 16)
                    else:
                        sp.dma_start(a_raw[:, :, 0:RANK],
                                     mixed_A[ph].rearrange("p k (b r) -> b p k r", r=RANK)[i + 1]).then_inc(a_in, 16)
                if ph == 0 and j in (1, 2):
                    sp.wait_ge(bmix_copied, 2 * i + j)
                    sp.dma_start(mixed_B.rearrange("p k (q m) -> q p k m", m=P)[2 * i + j - 1],
                                 b_stage.rearrange("p (k m) -> p k m", k=RK)).then_inc(bmix_out, 16)
                if ph == 0 and last and j == 0:
                    sp.wait_ge(bs_copied, 1)
                    for k in range(4):
                        sp.dma_start(shared_B.rearrange("r (j k m) -> k r j m", k=4, m=P)[k],
                                     Bs_out[k * RANK:(k + 1) * RANK].rearrange("r (j m) -> r j m", m=P)
                                     ).then_inc(bs_out, 16)
                sp.wait_ge(out_copied, CREDIT + t + 1)
                sp.dma_start(out[n], stage[:]).then_inc(stored, 16)
                if ph == 0 and last and j == 3:
                    load_bias(1)
                    sp.wait_ge(ax_stored, 16 * (CREDIT + NS))
                    sp.dma_start(ax_prev[:], partial_ax[0]).then_inc(axp_in, 16)
                    sp.wait_ge(w_lo_ready, 8 * NCH)
                    sp.wait_ge(bs_out, 64)
                    sp.wait_ge(bmix_out, 16 * (CREDIT + 16))
                    for rows in (RANK, R2 + RANK):
                        sp.dma_start(w_raw[rows:rows + RANK, :], shared_B).then_inc(bs_in, 16)

            phases(sp, step)
            sp.wait_ge(stored, 16 * (CREDIT + 2 * NS))

        @block.gpsimd
        def _(pool):
            nc.gpsimd.memset(ident[:], 0.0).then_inc(id_ready, 1)
            pool.wait_ge(id_ready, 1)
            nc.gpsimd.affine_select(out=ident[:], in_=ident[:], compare_op=ALU.not_equal, fill=1.0, base=0,
                                    pattern=[[-1, P]], channel_multiplier=1).then_inc(id_ready, 1)

            pool.wait_ge(bias_in, 32)
            with pool.Fori(0, NB) as i:
                for j in range(SPB):
                    pool.wait_ge(part_in, 16 * (4 * i + j + 1))
                    nc.gpsimd.tensor_tensor(stage[:, 0:HALF], stage[:, 0:HALF], bias_half[:], ALU.add).then_inc(pre_added, 1)
                    pool.wait_ge(x_in[j], 16 * (8 + i + 1))
                    nc.gpsimd.tensor_tensor(stage[:, HALF:L], stage[:, HALF:L], x_raw[:, j, PAD:XW], ALU.add
                                            ).then_inc(pre_added, 1)

        @block.scalar
        def _(act):
            def load_w(k):
                if k >= 4:
                    act.wait_ge(w_lo_ready, k - 3)
                c = k // 4 % NCH
                act.dma_start(w_stage[k % 4], W_v[k // (4 * NCH), c // S4, c % S4, k % 4]).then_inc(w_in[k % 4], 16)

            def split_w(k):
                c = k // 4
                act.wait_ge(w_in[k % 4], 16 * (c + 1))
                if c == 2 * NCH - 1:
                    act.wait_ge(ffn_done, NS)
                elif c >= NCH:
                    act.wait_ge(w_chunk_used, c % NCH + 1)
                nc.scalar.copy(w_hi[:, c % NCH, k % 4 * WP:(k % 4 + 1) * WP], w_stage[k % 4]).then_inc(w_hi_ready, 1)

            def split_pieces(first, end, phase_end):
                for k in range(first, end):
                    split_w(k)
                    if k + 3 < phase_end:
                        load_w(k + 3)

            def x_rearrange(slot, in_value, t_plus_1, ph, first=False):
                act.wait_ge(x_in[slot], in_value)
                if not first:
                    act.wait_ge(x_lo_ready, t_plus_1 - 1)
                else:
                    act.wait_ge(edge_zero, 1)
                for g in range(2):
                    for r in range(S4):
                        ins = nc.scalar.copy(x_quads[r * GC:(r + 1) * GC, g, 1 - ph:1 - ph + NQ + 1],
                                             x_raw[g * GC:(g + 1) * GC, slot, r:XW:S4])
                ins.then_inc(xq_act, 1)

            def x_split(t_plus_1, first=False):
                act.wait_ge(xq_act, t_plus_1)
                act.wait_ge(xq_dve, t_plus_1)
                if not first:
                    act.wait_ge(conv_done, t_plus_1 - 1)
                nc.scalar.copy(x_hi[:], x_quads).then_inc(x_hi_ready, 1)

            def y_split(t_plus_1):
                act.wait_ge(turn_done, t_plus_1)
                nc.scalar.copy(y_hi_out, turned).then_inc(y_hi_ready, 1)

            def a_split(k_plus_1):
                act.wait_ge(a_in, 16 * k_plus_1)
                if type(k_plus_1) is int and k_plus_1 == NB + 1:
                    act.wait_ge(a_lo_ready, NB)
                    nc.scalar.copy(a_raw[:, :, RANK:R2], as_next[:]).then_inc(as_switched, 1)
                    act.wait_ge(as_switched, 1)
                nc.scalar.copy(a_parts[:, :, 0:R2], a_raw[:]).then_inc(a_hi_ready, 1)

            def a_mixed_copy(ph):
                act.wait_ge(la_block_used, RK * (ph + 1))
                if ph == 0:
                    act.wait_ge(as_done, 1)
                else:
                    act.wait_ge(amix_out, 16)
                nc.scalar.copy(a_stage[:, 0:HALF], a_mixed[:, 0:HALF]).then_inc(amix_act, 1)

            x_rearrange(0, 16, 1, 0, first=True)
            act.wait_ge(cwt_done, 1)
            for d in range(3):
                ins = nc.scalar.copy(cw_hi[:, d].rearrange("p g (s o) -> p s g o", s=S4),
                                     cps[:, d, :].rearrange("p (s g o) -> p s g o", s=S4, g=GR))
            ins.then_inc(cw_hi_ready, 1)
            x_split(1, first=True)
            for k in range(3):
                load_w(k)
            split_pieces(0, 8, 4 * NCH)
            a_mixed_copy(0)
            x_rearrange(1, 16, 2, 0)
            x_split(2)
            a_split(1)
            y_split(1)
            split_pieces(8, 12, 4 * NCH)
            a_mixed_copy(1)
            split_pieces(12, 4 * NCH, 4 * NCH)

            def step(i, ph, j):
                t = 32 * ph + 4 * i + j
                last = type(i) is int
                act.wait_ge(ax_done, t + 1)
                act.wait_ge(ax_ready, CREDIT + t)
                nc.scalar.copy(ax_tmp[0:R2, :], ax_ps[R2:P, :])
                nc.scalar.copy(ax_tmp[R2:P, :], ax_ps[0:R2, :]).then_inc(ax_upper, 1)
                more = not (ph == 1 and last)
                if more or j < 2:
                    nph = 1 if last and j >= 2 else ph
                    x_rearrange((j + 2) % 4, 16 * (8 * ph + i + (j + 2) // 4 + 1), t + 3, nph)
                    x_split(t + 3)
                if j == 3 and more:
                    a_split(8 * ph + i + 2)
                if ph == 0 and j in (1, 2):
                    act.wait_ge(lb_raw_in, 16 * (2 * i + j))
                    nc.scalar.copy(lora_B_perm.rearrange("p k (n r) -> p k n r", r=R8),
                                   lora_B_raw.rearrange("p (n k r) -> p k n r", k=RK, r=R8)).then_inc(lb_perm, 1)
                    act.wait_ge(bt_done, 2 * i + j)
                    nc.scalar.copy(b_turn, cps[:, 0, :]).then_inc(bt_ready, 1)
                if ph == 0 and last and j == 0:
                    act.wait_ge(bs_done, 1)
                    act.wait_ge(bmix_out, 16 * (CREDIT + 14))
                    nc.scalar.copy(Bs_out, cps[:, 1, :]).then_inc(bs_copied, 1)
                if ph == 0 and last and j == 3:
                    act.wait_ge(bmix_out, 16 * (CREDIT + 16))
                    for k in range(3):
                        load_w(4 * NCH + k)
                    split_pieces(4 * NCH, 4 * (NCH + W_EARLY), 8 * NCH)
                if ph == 1:
                    act.wait_ge(ax_ready, CREDIT + t + 1)
                    nc.scalar.copy(ax_hi[:], ax[:]).then_inc(ax_hi_ready, 1)
                if ph == 1 and j == 0:
                    act.wait_ge(b_in, 32 * (i + 1))
                    act.wait_ge(bs_in, 32)
                    nc.scalar.copy(b_parts[:], w_raw[:]).then_inc(b_hi_ready, 1)
                if more or j < 3:
                    y_split(t + 2)
                if ph == 0 and last and j == 3:
                    split_pieces(4 * (NCH + W_EARLY), 8 * NCH, 8 * NCH)

            phases(act, step)

        @block.vector
        def _(dve):
            credit(dve, (out_copied, 1), (ax_ready, 1))
            V = nc.vector

            def split_w(k):
                dve.wait_ge(w_hi_ready, k + 1)
                c, cols = k // 4 % NCH, slice(k % 4 * WP, (k % 4 + 1) * WP)
                V.tensor_tensor(w_lo[:, c, cols], w_stage[k % 4], w_hi[:, c, cols].bitcast(F32),
                                ALU.subtract).then_inc(w_lo_ready, 1)

            def x_rearrange(slot, in_value, t_plus_1, ph, first=False):
                dve.wait_ge(x_in[slot], in_value)
                if not first:
                    dve.wait_ge(x_hi_ready, t_plus_1 - 1)
                    dve.wait_ge(x_lo_ready, t_plus_1 - 1)
                for g in range(2, GR):
                    for r in range(S4):
                        ins = V.tensor_copy(x_quads[r * GC:(r + 1) * GC, g, 1 - ph:1 - ph + NQ + 1],
                                            x_raw[g * GC:(g + 1) * GC, slot, r:XW:S4])
                ins.then_inc(xq_dve, 1)

            def x_split(t_plus_1):
                dve.wait_ge(xq_dve, t_plus_1)
                dve.wait_ge(x_hi_ready, t_plus_1)
                V.tensor_tensor(x_lo[:], x_quads, x_hi[:].bitcast(F32), ALU.subtract).then_inc(x_lo_ready, 1)

            def conv_copy(n, t_plus_1):
                dve.wait_ge(conv_done, t_plus_1)
                bias = ctx_bias[:, n, :].unsqueeze(2).to_broadcast([P, GR, NQ])
                V.tensor_tensor(conv_out, conv_ps, bias, ALU.add).then_inc(conv_copied, 1)

            def y_split(t_plus_1):
                dve.wait_ge(y_hi_ready, t_plus_1)
                V.tensor_tensor(y_lo_out, turned, y_hi_in, ALU.subtract).then_inc(y_lo_ready, 1)

            def a_split(k_plus_1):
                dve.wait_ge(a_hi_ready, k_plus_1)
                V.tensor_tensor(a_parts[:, :, R2:2 * R2], a_raw[:], a_parts[:, :, 0:R2].bitcast(F32),
                                ALU.subtract).then_inc(a_lo_ready, 1)

            V.memset(wpad, 0.0).then_inc(wpad_zero, 1)
            V.memset(x_quads[:, :, 0:1], 0.0).then_inc(edge_zero, 1)
            dve.wait_ge(conv_w_in, 16)
            dve.wait_ge(wpad_zero, 1)
            V.tensor_copy(wpad[:, 3:3 + TAPS, :], wraw).then_inc(wpad_ready, 1)
            dve.wait_ge(id_ready, 2)
            V.tensor_reduce(rep[:], ident[:].rearrange("p (a r) -> p r a", r=R8), AX_X, ALU.add).then_inc(rep_ready, 1)
            x_rearrange(0, 16, 1, 0, first=True)
            dve.wait_ge(small_in, 16 * 7)
            V.tensor_copy(gate_exp.rearrange("b (n r) -> b n r", r=R8),
                          gate_sb[:].unsqueeze(2).to_broadcast([NB, NL, R8])).then_inc(gexp_ready, 1)
            dve.wait_ge(ctxt_done, 1)
            V.tensor_copy(cwT4.rearrange("p (g s o) -> p g s o", g=GR, s=S4),
                          acc[:, 0, 0:CH].rearrange("p (g o) -> p g o", g=GR).unsqueeze(2).to_broadcast([P, GR, S4, GC])
                          ).then_inc(ctxt_ready, 1)
            V.tensor_copy(condT, acc[:, 0, CH:CH + NS]).then_inc(ctxt_ready, 1)
            dve.wait_ge(gcol_done, 1)
            V.tensor_copy(gate_col[:], acc[:, 1, 0:NB]).then_inc(gcol_ready, 1)
            dve.wait_ge(gcol_ready, 1)
            dve.wait_ge(rep_ready, 1)
            V.tensor_tensor(G[:], gate_col[:].unsqueeze(2).to_broadcast([P, NB, R8]),
                            rep[:].unsqueeze(1).to_broadcast([P, NB, R8]), ALU.mult).then_inc(g_ready, 1)
            dve.wait_ge(cw_hi_ready, 1)
            for d in range(3):
                ins = V.tensor_tensor(cw_lo[:, d].rearrange("p g (s o) -> p s g o", s=S4),
                                      cps[:, d, :].rearrange("p (s g o) -> p s g o", s=S4, g=GR),
                                      cw_hi[:, d].bitcast(F32).rearrange("p g (s o) -> p s g o", s=S4), ALU.subtract)
            ins.then_inc(cw_lo_ready, 1)
            dve.wait_ge(edge_zero, 1)
            x_split(1)
            for k in range(8):
                split_w(k)
            dve.wait_ge(ctx_done, 1)
            V.tensor_tensor(ctx_bias[:].rearrange("p n g -> p g n"),
                            acc[:, 2, 0:P].rearrange("p (g n) -> p g n", g=GR),
                            bias_col[:].unsqueeze(2).to_broadcast([P, GR, NS]), ALU.add).then_inc(ctx_ready, 1)
            dve.wait_ge(as_done, 1)
            V.tensor_copy(a_raw[:, :, RANK:R2], cps[:, 3, 0:NCH * RANK].rearrange("p (k r) -> p k r", r=RANK)
                          ).then_inc(as_copied, 1)
            V.tensor_copy(as_next[:], cps[:, 3, NCH * RANK:2 * NCH * RANK].rearrange("p (k r) -> p k r", r=RANK)
                          ).then_inc(as_copied, 1)

            def a_mixed_copy(ph):
                dve.wait_ge(la_block_used, RK * (ph + 1))
                if ph == 1:
                    dve.wait_ge(amix_out, 16)
                V.tensor_copy(a_stage[:, HALF:L], a_mixed[:, HALF:L]).then_inc(amix_dve, 1)

            a_mixed_copy(0)
            dve.wait_ge(amix_act, 1)
            V.tensor_copy(a_raw[:, :, 0:RANK], a_mixed.rearrange("p (k n) -> p k n", k=NCH)[:, :, 0:RANK]).then_inc(a_in, 16)
            dve.wait_ge(ctx_ready, 1)
            conv_copy(0, 1)
            x_rearrange(1, 16, 2, 0)
            x_split(2)
            a_split(1)
            y_split(1)
            for k in range(8, 12):
                split_w(k)
            a_mixed_copy(1)
            for k in range(12, 4 * NCH):
                split_w(k)

            def step(i, ph, j):
                t = 32 * ph + 4 * i + j
                n = 4 * i + j
                last = type(i) is int
                more = not (ph == 1 and last)
                if more or j < 3:
                    conv_copy((n + 1) if not (last and j == 3) else 0, t + 2)
                dve.wait_ge(ax_upper, t + 1)
                V.tensor_tensor(ax_tmp[:], ax_ps, ax_tmp[:], ALU.add).then_inc(ax_sum, 1)
                dve.wait_ge(ax_sum, t + 1 if ph == 0 else NS + 2 * n + 1)
                if ph == 0:
                    dve.wait_ge(ax_stored, 16 * (CREDIT + t))
                    V.tensor_tensor(ax[:], ax_tmp[:, 0:P], ax_tmp[:, P:2 * P], ALU.add).then_inc(ax_ready, 1)
                else:
                    V.tensor_tensor(ax_tmp[:, 0:P], ax_tmp[:, 0:P], ax_tmp[:, P:2 * P], ALU.add).then_inc(ax_sum, 1)
                    dve.wait_ge(axp_in, 16 * (4 * i + j + 1))
                    dve.wait_ge(ax_stored, 16 * (CREDIT + NS))
                    dve.wait_ge(ax_sum, NS + 2 * (4 * i + j) + 2)
                    V.tensor_tensor(ax[:], ax_tmp[:, 0:P], ax_prev[:], ALU.add).then_inc(ax_ready, 1)
                if more or j < 2:
                    nph = 1 if last and j >= 2 else ph
                    if ph == 0 and last and j == 2:
                        dve.wait_ge(x_hi_ready, t + 2)
                        dve.wait_ge(x_lo_ready, t + 2)
                        V.memset(x_quads[:, :, XQ - 1:XQ], 0.0).then_inc(edge_zero, 1)
                    x_rearrange((j + 2) % 4, 16 * (8 * ph + i + (j + 2) // 4 + 1), t + 3, nph)
                    if ph == 0 and last and j == 2:
                        dve.wait_ge(edge_zero, 2)
                    x_split(t + 3)
                if j == 3 and more:
                    a_split(8 * ph + i + 2)
                if ph == 0 and last and j == 3:
                    for k in range(4 * NCH, 4 * (NCH + W_EARLY)):
                        split_w(k)
                if ph == 0 and j in (1, 2):
                    dve.wait_ge(bmix_out, 16 * (CREDIT + 2 * i + j - 1))
                    if last and j == 1:
                        dve.wait_ge(bs_out, 64)
                    dve.wait_ge(bmix_done, 2 * i + j)
                    V.tensor_copy(b_stage, cps[0:NB * R8, 1, :]).then_inc(bmix_copied, 1)
                if ph == 1:
                    dve.wait_ge(ax_hi_ready, 4 * i + j + 1)
                    V.tensor_tensor(ax_lo[:], ax[:], ax_hi[:].bitcast(F32), ALU.subtract).then_inc(ax_lo_ready, 1)
                if ph == 1 and j == 0:
                    dve.wait_ge(b_hi_ready, i + 1)
                    V.tensor_tensor(b_parts[R2:P, :], w_raw[R2:P, :], b_parts[R2:P, :].bitcast(F32), ALU.subtract
                                    ).then_inc(b_lo_ready, 1)
                dve.wait_ge(ffn_done, t + 1)
                if ph == 0:
                    dve.wait_ge(stored, 16 * (CREDIT + t))
                    dve.wait_ge(bias_in, 16)
                    V.tensor_tensor(stage[:, 0:HALF], acc[:, 0:2, :].rearrange("p a n -> p (a n)"),
                                    x_raw[:, j, 0:HALF], ALU.add)
                    V.tensor_tensor(stage[:, HALF:L], acc[:, 2:4, :].rearrange("p a n -> p (a n)"),
                                    bias_half[:], ALU.add).then_inc(out_copied, 1)
                else:
                    dve.wait_ge(pre_added, 2 * (4 * i + j + 1))
                    V.tensor_tensor(stage[:], acc[:].rearrange("p a n -> p (a n)"), stage[:], ALU.add
                                    ).then_inc(out_copied, 1)
                if more or j < 3:
                    y_split(t + 2)
                if ph == 0 and last and j == 3:
                    for k in range(4 * (NCH + W_EARLY), 8 * NCH):
                        split_w(k)

            phases(dve, step)

        @block.tensor
        def _(pe):
            T = nc.tensor

            def conv(t_plus_1):
                pe.wait_ge(x_lo_ready, t_plus_1)
                for g in range(GR):
                    n = 0
                    for d in range(3):
                        for wt, xt in ((cw_hi, x_hi), (cw_hi, x_lo), (cw_lo, x_hi)):
                            ins = T.matmul(conv_ps[:, g, :], wt[:, d, g, :], xt[:, g, d:d + NQ],
                                           start=(n == 0), stop=(n == 8))
                            n += 1
                ins.then_inc(conv_done, 1)

            def turn(t_plus_1):
                pe.wait_ge(conv_copied, t_plus_1)
                for g in range(GR):
                    for c in range(QC):
                        ins = T.transpose(turn_ps[:, g, c * P:(c + 1) * P], conv_out[:, g, c * P:(c + 1) * P],
                                          ident[:])
                ins.then_inc(turn_done, 1)

            pe.wait_ge(id_ready, 2)
            pe.wait_ge(wpad_ready, 1)
            wp = wpad.rearrange("p k i -> p (k i)")
            for d in range(3):
                for s in range(S4):
                    k0 = (4 * d + 3 - s) * GC
                    ins = T.transpose(cps[:, d, s * P:(s + 1) * P], wp[:, k0:k0 + P], ident[:])
            ins.then_inc(cwt_done, 1)
            pe.wait_ge(small_in, 16 * 7)
            T.transpose(acc[:, 0, 0:CH], cw_raw, ident[:])
            T.transpose(acc[:, 0, CH:CH + NS], cond_raw, ident[0:NS, 0:NS]).then_inc(ctxt_done, 1)
            pe.wait_ge(gexp_ready, 1)
            T.matmul(acc[:, 1, 0:NB], gate_exp, ident[0:NB, 0:NB], start=True, stop=True).then_inc(gcol_done, 1)
            pe.wait_ge(ctxt_ready, 2)
            for g in range(GR):
                ins = T.matmul(acc[:, 2, g * NS:(g + 1) * NS], cwT4[:, g * P:(g + 1) * P], condT, start=True, stop=True)
            ins.then_inc(ctx_done, 1)
            pe.wait_ge(cw_lo_ready, 1)
            conv(1)
            pe.wait_ge(as_raw_in, 16)
            for ch in range(2 * NCH):
                l0 = ch // S4 * 512 + ch % S4
                ins = T.transpose(cps[:, 3, ch * RANK:(ch + 1) * RANK], As_raw[:, l0:l0 + 509:S4], ident[0:RANK, 0:RANK])
            ins.then_inc(as_done, 1)

            def mix_A(ph):
                by_block = a_mixed.rearrange("p (c b r k) -> p c k b r", c=NCH, b=NB, k=RK)
                for k in range(RK):
                    n = ph * RK + k
                    pe.wait_ge(la_raw_in[n % 2], 16 * (n // 2 + 1))
                    for ch in range(NCH):
                        l0 = ch // S4 * 512 + ch % S4
                        ins = T.matmul(by_block[:, ch, k], lora_A_raw[n % 2][:, l0:l0 + 509:S4],
                                       G[:].rearrange("p b r -> p (b r)"), start=True, stop=True)
                    ins.then_inc(la_block_used, 1)

            pe.wait_ge(g_ready, 1)
            pe.wait_ge(ctx_ready, 1)
            mix_A(0)
            pe.wait_ge(as_copied, 2)
            turn(1)
            conv(2)
            pe.wait_ge(a_in, 16)
            mix_A(1)
            pe.wait_ge(amix_act, 2)
            pe.wait_ge(amix_dve, 2)

            def mix_B(i, j, last, ch):
                if ch == 4 and j in (1, 2):
                    pe.wait_ge(lb_perm, 2 * i + j)
                    pe.wait_ge(conv_copied, 4 * i + j + 2)
                    for k in range(RK):
                        ins = T.transpose(cps[:, 0, k * P:(k + 1) * P], lora_B_perm[:, k, :], ident[:])
                    ins.then_inc(bt_done, 1)
                if ch == 6 and j in (1, 2):
                    pe.wait_ge(bt_ready, 2 * i + j)
                    ins = T.matmul(cps[0:NB * R8, 1, :], G[:].rearrange("p b r -> p (b r)"), b_turn, start=True, stop=True)
                    ins.then_inc(bmix_done, 1)
                if ch == 4 and j == 0 and last:
                    pe.wait_ge(bs_raw_in, 16)
                    pe.wait_ge(conv_copied, 4 * i + j + 2)
                    for k in range(4):
                        ins = T.transpose(cps[:, 1, k * P:(k + 1) * P], Bs_raw[:, k * P:(k + 1) * P], ident[:])
                    ins.then_inc(bs_done, 1)

            def step(i, ph, j):
                t = 32 * ph + 4 * i + j
                last = type(i) is int
                more = not (ph == 1 and last)
                if j == 0:
                    pe.wait_ge(a_lo_ready, 8 * ph + i + 1)
                pe.wait_ge(y_lo_ready, t + 1)
                for ch in range(NCH):
                    ins = T.matmul(ax_ps, a_parts[:, ch, :], y_t[:, ch].rearrange("p h r -> p (h r)"),
                                   start=(ch == 0), stop=(ch == NCH - 1))
                ins.then_inc(ax_done, 1)
                pe.wait_ge(out_copied, CREDIT + t)
                for ch in range(NCH):
                    if j == 0:
                        pe.wait_ge(w_lo_ready, 4 * (NCH * ph + ch + 1))
                    for part, wt in ((0, w_hi), (0, w_lo), (1, w_hi)):
                        for m in range(MB):
                            ins = T.matmul(acc[:, m, :], y_t[:, ch, part, :], wt[:, ch, m * 512:(m + 1) * 512],
                                           start=(ch == 0 and part == 0 and wt is w_hi),
                                           stop=(ph == 0 and ch == NCH - 1 and part == 1))
                    if ph == 0:
                        mix_B(i, j, last, ch)
                    if ph == 0 and last and j == 3:
                        if ch < NCH - 1:
                            ins.then_inc(w_chunk_used, 1)
                if ph == 0:
                    ins.then_inc(ffn_done, 1)
                else:
                    pe.wait_ge(ax_lo_ready, 4 * i + j + 1)
                    if j == 0:
                        pe.wait_ge(b_lo_ready, i + 1)
                    for part in (ax_hi, ax_lo):
                        for m in range(MB):
                            ins = T.matmul(acc[:, m, :], part[:], b_parts[:, m * 512:(m + 1) * 512],
                                           start=False, stop=(part is ax_lo))
                    ins.then_inc(ffn_done, 1)
                if more or j < 3:
                    pe.wait_ge(ax_ready, CREDIT + t + 1)
                    turn(t + 2)
                if more or j < 2:
                    if ph == 0 and j in (1, 2):
                        pe.wait_ge(bmix_copied, 2 * i + j)
                    if ph == 0 and last and j == 0:
                        pe.wait_ge(bs_copied, 1)
                    conv(t + 3)

            phases(pe, step)


INPUTS = ["x", "cond_128", "fside_S_0", "L0_cond_weight", "L0_cond_c_weight", "L0_ffn_gate", "L0_ffn_kernel",
          "L0_ffn_bias", "L0_ffn_lora_A", "L0_ffn_lora_B", "L0_ffn_lora_A_shared", "L0_ffn_lora_B_shared"]


def kernel(**inputs):
    import numpy as np
    import concourse.bacc as bacc
    from concourse.bass_utils import run_bass_kernel_spmd

    nc = bacc.Bacc("TRN2", target_bir_lowering=False, num_devices=1, dynamic_dma_scratch_size=1024)
    arrays, aps = {}, []
    for name in INPUTS:
        a = np.ascontiguousarray(inputs[name])
        arrays[f"in_{name}"] = a
        aps.append(nc.dram_tensor(f"in_{name}", a.shape, mybir.dt.from_np(a.dtype), kind="ExternalInput").ap())
    out = nc.dram_tensor("out", (NS, CH, L), F32, kind="ExternalOutput").ap()
    build(nc, *aps, out)
    r = run_bass_kernel_spmd(nc, [arrays], core_ids=[0])
    return r.results[0]["out"]
```
